# Optimizing a Trainium2 kernel written in Bass

```python
import numpy as np
import jax
import jax.numpy as jnp

def _softmax(x, axis=-1):
    return jax.nn.softmax(x, axis=axis)

def _gelu(x):
    return jax.nn.gelu(x, approximate=True)

def _silu(x):
    return jax.nn.silu(x)

def _sigmoid(x):
    return jax.nn.sigmoid(x)

def _layernorm(x, axis=-1, eps=1e-05):
    m = jnp.mean(x, axis=axis, keepdims=True)
    v = jnp.var(x, axis=axis, keepdims=True)
    return (x - m) / jnp.sqrt(v + eps)

def _scatter_add(tgt, idx, src, axis=0):
    return tgt.at[idx].add(src)

def _segment_sum(src, seg, n):
    return jax.ops.segment_sum(src, seg, n)
kernel_name = 'mk_seq_postln_d1_jaxref_r8_e2594e'

def setup_inputs(seed: int=0):
    np.random.seed(seed)
    _w = jnp.asarray

    def _L0_attn_setup():
        import jax, jax.numpy as jnp
        import numpy as np
        D = 128
        H = 16
        DH = D // H
        B, N = (4, 128)
        key = jax.random.key(seed)
        k0, k1, k2 = jax.random.split(key, 3)
        x = jax.random.normal(k0, (B, N, D), jnp.float32)
        Wkqv = jax.random.normal(k1, (H, D, 2 * D + DH), jnp.float32) * 0.02
        bkqv = jnp.zeros((H, 2 * D + DH), jnp.float32)
        Wp = jax.random.normal(k2, (D, D), jnp.float32) * 0.02
        bp = jnp.zeros((D,), jnp.float32)
        return {'x': x, 'Wkqv': Wkqv, 'bkqv': bkqv, 'Wp': Wp, 'bp': bp}
    _L0_attn_in = _L0_attn_setup()

    def _L0_ffn_setup():
        import jax, jax.numpy as jnp
        import numpy as np
        B, S, D, E, H, K = (4, 256, 128, 8, 512, 2)
        EPS = 1e-06

        def _ln(x, scale, bias):
            m = jnp.mean(x, axis=-1, keepdims=True)
            v = jnp.mean(jnp.square(x - m), axis=-1, keepdims=True)
            return (x - m) * jax.lax.rsqrt(v + EPS) * scale + bias
        key = jax.random.key(seed)
        ks = jax.random.split(key, 4)
        s1 = 1.0 / np.sqrt(D)
        s2 = 1.0 / np.sqrt(H)
        return {'x': jax.random.normal(ks[0], (B, S, D), jnp.float32), 'router_ln_scale': jnp.ones((D,), jnp.float32), 'router_ln_bias': jnp.zeros((D,), jnp.float32), 'router_w': jax.random.normal(ks[1], (E, D), jnp.float32) * s1, 'router_b': jnp.zeros((E,), jnp.float32), 'expert_ln_scale': jnp.ones((E, D), jnp.float32), 'expert_ln_bias': jnp.zeros((E, D), jnp.float32), 'w1': jax.random.normal(ks[2], (E, H, D), jnp.float32) * s1, 'b1': jnp.zeros((E, H), jnp.float32), 'w2': jax.random.normal(ks[3], (E, D, H), jnp.float32) * s2, 'b2': jnp.zeros((E, D), jnp.float32)}
    _L0_ffn_in = _L0_ffn_setup()
    _d = {'L0_attn_x': _L0_attn_in['x'], 'L0_attn_Wkqv': _L0_attn_in['Wkqv'], 'L0_attn_bkqv': _L0_attn_in['bkqv'], 'L0_attn_Wp': _L0_attn_in['Wp'], 'L0_attn_bp': _L0_attn_in['bp'], 'L0_ffn_router_ln_scale': _L0_ffn_in['router_ln_scale'], 'L0_ffn_router_ln_bias': _L0_ffn_in['router_ln_bias'], 'L0_ffn_router_w': _L0_ffn_in['router_w'], 'L0_ffn_router_b': _L0_ffn_in['router_b'], 'L0_ffn_expert_ln_scale': _L0_ffn_in['expert_ln_scale'], 'L0_ffn_expert_ln_bias': _L0_ffn_in['expert_ln_bias'], 'L0_ffn_w1': _L0_ffn_in['w1'], 'L0_ffn_b1': _L0_ffn_in['b1'], 'L0_ffn_w2': _L0_ffn_in['w2'], 'L0_ffn_b2': _L0_ffn_in['b2']}
    _x0 = _d['L0_attn_x']
    _d['L0_attn_x'] = jax.random.normal(jax.random.fold_in(jax.random.key(seed), 1), (4, 512, 128), dtype=_x0.dtype)
    del _x0
    return _d

def reference(L0_attn_x, L0_attn_Wkqv, L0_attn_bkqv, L0_attn_Wp, L0_attn_bp, L0_ffn_router_ln_scale, L0_ffn_router_ln_bias, L0_ffn_router_w, L0_ffn_router_b, L0_ffn_expert_ln_scale, L0_ffn_expert_ln_bias, L0_ffn_w1, L0_ffn_b1, L0_ffn_w2, L0_ffn_b2):

    def _L0_attn_ref(x, Wkqv, bkqv, Wp, bp):
        import jax, jax.numpy as jnp
        import numpy as np
        D = 128
        H = 16
        DH = D // H
        B, N = (4, 128)
        Bm, Nm, Dm = x.shape
        y = jnp.einsum('bnd,hde->bhne', x, Wkqv) + bkqv[None, :, None, :]
        k = y[..., :Dm]
        q = y[..., Dm:2 * Dm]
        v = y[..., 2 * Dm:]
        A = jnp.einsum('bhnd,bhmd->bhnm', q, k) / jnp.sqrt(jnp.float32(Dm))
        mask = jnp.tril(jnp.ones((Nm, Nm), dtype=bool))
        A = jnp.where(mask[None, None], A, -jnp.inf)
        A = jax.nn.softmax(A, axis=-1)
        sa = jnp.einsum('bhnm,bhmd->bnhd', A, v).reshape(Bm, Nm, Dm)
        return sa @ Wp + bp

    def _L0_ffn_ref(x, router_ln_scale, router_ln_bias, router_w, router_b, expert_ln_scale, expert_ln_bias, w1, b1, w2, b2):
        import jax, jax.numpy as jnp
        import numpy as np
        B, S, D, E, H, K = (4, 256, 128, 8, 512, 2)
        EPS = 1e-06

        def _ln(x, scale, bias):
            m = jnp.mean(x, axis=-1, keepdims=True)
            v = jnp.mean(jnp.square(x - m), axis=-1, keepdims=True)
            return (x - m) * jax.lax.rsqrt(v + EPS) * scale + bias
        orig_shape = x.shape
        xf = x.reshape(-1, D)
        T = xf.shape[0]
        logits = _ln(xf, router_ln_scale, router_ln_bias) @ router_w.T + router_b
        probs = jax.nn.softmax(logits, axis=-1)
        topw, topi = jax.lax.top_k(probs, K)
        topw = topw / jnp.sum(topw, axis=-1, keepdims=True)
        gates = jnp.zeros((T, E), xf.dtype).at[jnp.arange(T)[:, None], topi].set(topw)

        def expert(ls, lb, W1, B1, W2, B2):
            h = jax.nn.gelu(_ln(xf, ls, lb) @ W1.T + B1, approximate=False)
            return h @ W2.T + B2
        ys = jax.vmap(expert)(expert_ln_scale, expert_ln_bias, w1, b1, w2, b2)
        out = jnp.einsum('te,etd->td', gates, ys)
        return out.reshape(orig_shape)
    x = L0_attn_x
    x = _layernorm(x + _L0_attn_ref(x, L0_attn_Wkqv, L0_attn_bkqv, L0_attn_Wp, L0_attn_bp), axis=-1)
    x = _layernorm(x + _L0_ffn_ref(x, L0_ffn_router_ln_scale, L0_ffn_router_ln_bias, L0_ffn_router_w, L0_ffn_router_b, L0_ffn_expert_ln_scale, L0_ffn_expert_ln_bias, L0_ffn_w1, L0_ffn_b1, L0_ffn_w2, L0_ffn_b2), axis=-1)
    return x

_drawn_inputs = setup_inputs


def setup_inputs(seed=0):
    import zlib

    import numpy as np

    out = dict(_drawn_inputs(seed))
    spreads = {'L0_attn_bkqv': (0.0, 0.1),
     'L0_attn_bp': (0.0, 0.1),
     'L0_ffn_router_ln_scale': (1.0, 0.2),
     'L0_ffn_router_ln_bias': (0.0, 0.1),
     'L0_ffn_router_b': (0.0, 0.1),
     'L0_ffn_expert_ln_scale': (1.0, 0.2),
     'L0_ffn_expert_ln_bias': (0.0, 0.1),
     'L0_ffn_b1': (0.0, 0.1),
     'L0_ffn_b2': (0.0, 0.1)}
    factors = {'L0_attn_Wkqv': 2.936}
    for name, (base, spread) in spreads.items():
        noise = np.random.default_rng([zlib.crc32(name.encode()), seed]).standard_normal(out[name].shape)
        drawn = base * np.exp(spread * noise) if base else spread * noise
        out[name] = jnp.asarray(drawn.astype(out[name].dtype))
    for name, factor in factors.items():
        out[name] = (out[name] * factor).astype(out[name].dtype)
    return out
```

```python
from contextlib import ExitStack

import numpy as np

import concourse.bass as bass
from concourse import mybir

B, N, D = 4, 512, 128
H, DH = 16, 8
E, HID = 8, 512
P = 128
JT = N // P
NT = B * JT
T = B * N
HC = HID // P
G = H * B
BLK = JT * (JT + 1) // 2
SC = BLK * P
VW = 3 * DH + 1
VS = 32
VC = H * DH + H
EPS_LN, EPS_MOE = 1e-5, 1e-6
MASKED = -1e30
P_SCALE = float(np.log(64.0))
T_AT = {0: 0, 1: 4 * P, 3: 7 * P, 2: 8 * P}
R_AT = {3: (0, 0), 2: (1, 0), 0: (1, 3 * P), 1: (2, 0)}

C_BK, C_BQ, C_LS, C_LB, C_B2 = 0, H, 2 * H, 2 * H + E, 2 * H + 2 * E
C_B1 = C_B2 + E
C_RLS = C_B1 + E * HC
C_RLB = C_RLS + 1
C_RW = C_RLB + 1
C_ALL = C_RW + E


class Step:

    def __init__(self, rounds, r):
        self.rounds, self.r = rounds, r

    def at(self, lag):
        return Step(self.rounds, self.r - lag)

    @property
    def g(self):
        return self.rounds * 8 + self.r

    @property
    def real(self):
        return not isinstance(self.rounds, int) or 0 <= self.g < G

    @property
    def b(self):
        return self.r % B

    @property
    def head(self):
        return self.rounds * 2 + self.r // B

    @property
    def half(self):
        return self.rounds + self.r // (2 * B)

    @property
    def parity(self):
        return (self.r // B) % 2


FIRST_STEP, LOOP_STEP, LAST_STEP = -2, 4, G + 1


def attention_steps(eng, emit):
    for k in range(FIRST_STEP, LOOP_STEP):
        emit(Step(0, k))
    rounds = G // 8 - 1
    with eng.Fori(0, rounds) as i:
        for r in range(LOOP_STEP, LOOP_STEP + 8):
            emit(Step(i, r))
    for r in range(LOOP_STEP, LAST_STEP - 8 * rounds + 1):
        emit(Step(rounds, r))


def wait(eng, sem, value):
    if isinstance(value, int) and value <= 0:
        return
    eng.wait_ge(sem, value)


def post_ln_layer(nc, x, wkqv, bkqv, wp, bp, rls, rlb, rw, rb, els, elb, w1, b1, w2, b2, out):
    f32, f32r = mybir.dt.float32, mybir.dt.float32r
    bf16, f16 = mybir.dt.bfloat16, mybir.dt.float16
    ACT, ALU, AX = mybir.ActivationFunctionType, mybir.AluOpType, mybir.AxisListType

    gates_dram = nc.dram_tensor("gates_by_expert", [E, T], f32, kind="Internal").ap()

    ctx = ExitStack()
    early = ExitStack()
    with ctx:
        def sb(name, shape, dt, stack=ctx):
            return stack.enter_context(nc.sbuf_tensor(name, shape, dt))

        def sem(name):
            return ctx.enter_context(nc.semaphore(name))

        ident = sb("ident", [P, P], f32)
        ident16 = sb("ident16", [P, P], bf16)
        future = sb("future", [P, P], bf16)
        ones = sb("ones", [P, P], f32)
        onesr = sb("onesr", [P, P], f32r)
        p_bias = sb("p_bias", [P, 1], f32)
        zero_bias = sb("zero_bias", [P, 1], f32)
        neg_half = sb("neg_half", [P, JT], f32)
        order = sb("order", [P, E, E], f32)
        xs = sb("xs", [P, NT, D], f32)
        xt = [sb("xt_hi", [P, T], f32r), sb("xt_lo", [P, T], f32r)]
        cols = sb("cols", [P, C_ALL], f32)
        rw_s = [sb("rw_hi", [P, E], f32r), sb("rw_lo", [P, E], f32r)]
        rwf = sb("rwf", [P, E], f32)
        rbias = sb("rbias", [P, E], f32)
        rlb_b = sb("rlb_b", [P, P], f32)
        wp_s = sb("wp_s", [D, D], f32)
        lb_b = sb("lb_b", [P, E, D], f32)
        o_all = sb("o_all", [P, H, B, JT, VW], f32)

        t_s = [sb("t_hi", [P, 4, N], f32r, early), sb("t_lo", [P, 4, N], f32r, early)]
        m_cur = [sb(f"m_cur{p}", [P, 2, D], f32r, early) for p in range(2)]
        v_cur = [sb(f"v_cur{p}", [P, NT, VS], bf16, early) for p in range(2)]
        s_cur = [sb(f"s_cur{p}", [P, 1 + NT], f32, early) for p in range(2)]
        row_max = sb("row_max", [P, 4, JT], f32, early)
        row_tot = sb("row_tot", [P, 2, JT], f32, early)
        shift = sb("shift", [P, 2, JT], f32, early)
        diag = [sb(f"diag{p}", [P, JT, P], f32r, early) for p in range(2)]
        p32 = sb("p32", [P, 2, SC], f32, early)
        p_hi = sb("p_hi", [P, 2, SC], f16, early)
        p_lo = sb("p_lo", [P, 2, SC], f16, early)
        m_all = sb("m_all", [P, H, 2, D], f32r, early)
        v_all = sb("v_all", [P, H, NT, VS], bf16, early)
        s_all = sb("s_all", [P, H, 1 + NT], f32, early)
        rows = sb("rows", [C_ALL, P], f32, early)
        row1 = sb("row1", [1, H * DH + D + E], f32, early)
        w_raw = sb("w_raw", [D, 4, 2 * D + DH], f32, early)
        wv_raw = sb("wv_raw", [D, H, DH], f32, early)
        wkT = sb("wkT", [D, H, D + 1], f32, early)
        wqT = sb("wqT", [D, H, D], f32, early)
        bias_prod = sb("bias_prod", [P, H], f32, early)
        vc32 = sb("vc32", [P, VC], f32, early)
        vc = [sb("vc_hi", [P, VC], f32r, early), sb("vc_lo", [P, VC], f32r, early)]
        vc_bias = sb("vc_bias", [P, VC + D], f32, early)
        v32 = p32[:].rearrange("p a n -> p (a n)")[:, 0:NT * P].rearrange("p (t n) -> p t n", t=NT)
        early.close()

        a_num = sb("a_num", [P, 2, H, JT, DH], f32)
        a_den = sb("a_den", [P, 2, H, JT], f32)
        sa = sb("sa", [P, 2, JT, D], f32)
        saT = sb("saT", [P, 2, N], f32)
        x_pre = sb("x_pre", [P, 2, JT, D], f32)
        z = sb("z", [P, 2, JT, D], f32)
        bn6 = sb("bn6", [P, 2, JT, 6], f32)
        mv = sb("mv", [P, 2, JT, 2], f32)
        var_eps = sb("var_eps", [P, 2, JT], f32)
        rstd = sb("rstd", [P, 2, JT], f32)
        probs = sb("probs", [P, JT, E], f32)
        top = sb("top", [P, JT], f32)
        tot = sb("tot", [P, JT], f32)
        pair_gt = sb("pair_gt", [P, JT, E, E], f32)
        pair_eq = sb("pair_eq", [P, JT, E, E], f32)
        rank = sb("rank", [P, JT, E], f32)
        gates = sb("gates", [P, JT, E], f32)
        gatesT = sb("gatesT", [E, T], f32)
        w1_raw = [sb(f"w1_raw{p}", [P, HC, D], f32) for p in range(2)]
        w2_raw = [sb(f"w2_raw{p}", [D, HID], f32) for p in range(2)]
        w1_s = [[sb(f"w1_{n}{p}", [D, HID], f32r) for n in ("hi", "lo")] for p in range(2)]
        w2_s = [[sb(f"w2_{n}{p}", [P, HC, D], f32r) for n in ("hi", "lo")] for p in range(2)]
        w1_lb = sb("w1_lb", [P, HC, D], f32)
        w1_lb_sum = sb("w1_lb_sum", [P, HC], f32)
        b1_s = [sb(f"b1_s{p}", [P, HC], f32) for p in range(2)]
        gate_b = [sb(f"gate_b{p}", [P, T], f32) for p in range(2)]
        NH = 4
        h32 = sb("h32", [P, NH, N], f32)
        h_hi = sb("h_hi", [P, NH, N], f32r)
        h_lo = sb("h_lo", [P, NH, N], f32r)
        y_g = sb("y_g", [P, 2, N], f32)
        acc = sb("acc", [P, T], f32)
        x_out = sb("x_out", [P, 2, JT, D], f32)

        bank = [ctx.enter_context(nc.psum_tensor(f"bank{i}", [P, 512], f32)) for i in range(2)]
        ps_rows = ctx.enter_context(nc.psum_tensor("ps_rows", [P, 3, 512], f32))
        ps_sT = ctx.enter_context(nc.psum_tensor("ps_sT", [P, 3, 512], f32))
        ps_t, ps_o = bank
        banks = [ps_t[:, :], ps_o[:, :]] + [ps_rows[:, i, :] for i in range(3)] + [ps_sT[:, i, :] for i in range(3)]
        sT = ps_sT[:].rearrange("p a n -> p (a n)")[:, 0:SC]

        s_const = sem("const_ready")
        s_rows_in = sem("small_rows_loaded")
        s_x_in = [sem(f"x{b}_loaded") for b in range(B)]
        s_w_in = [sem(f"w{i}_loaded") for i in range(4)]
        s_misc_in = sem("row_biases_loaded")
        s_wv_in = sem("wv_loaded")
        s_wp_in = sem("wp_loaded")
        s_fill = sem("setup_bank_filled")
        s_sact = sem("setup_bank_read_by_scalar")
        s_sdve = sem("setup_bank_read_by_vector")
        s_vchain = sem("vector_chain")
        s_pchain = sem("pool_chain")
        s_v_all = sem("values_split")
        s_v1 = sem("v1_ready")
        s_vcw = sem("vc_split")
        s_v32 = sem("v32_ready")
        s_rw = sem("router_weights_ready")
        s_m = [sem(f"m_of_head_here{p}") for p in range(2)]
        s_s = [sem(f"constants_of_head_here{p}") for p in range(2)]
        s_v = [sem(f"v_of_head_here{p}") for p in range(2)]
        s_t, s_thi, s_tlo = sem("t_ready"), sem("t_hi_ready"), sem("t_lo_ready")
        s_rowsc, s_max, s_diag = sem("row_scores_ready"), sem("row_max_ready"), sem("diag_ready")
        s_shift = sem("shift_steps")
        s_sT, s_exp, s_mask = sem("scoresT_ready"), sem("exp_ready"), sem("mask_ready")
        s_seen = sem("exp_seen_by_pool")
        s_hi, s_lo, s_pv, s_o = sem("p_hi_ready"), sem("p_lo_ready"), sem("pv_ready"), sem("o_saved")

        block = ctx.enter_context(nc.Block())

        J_X, J_W, J_M, J_B, J_V = 1, 5, 13, 21, 22
        JOBS = J_V + NT // 2
        act_reads = [n < J_V and not (J_W <= n < J_M and (n - J_W) % 2) for n in range(JOBS)]
        dve_reads = [not (J_W <= n < J_M and (n - J_W) % 2 == 0) for n in range(JOBS)]

        def act_done(n):
            return sum(act_reads[:n + 1])

        def dve_done(n):
            return sum(dve_reads[:n + 1])

        s_sa, s_saT_ps, s_saT = sem("sa_ready"), sem("saT_in_bank"), sem("saT_ready")
        s_att, s_xpre = sem("attention_out_in_bank"), sem("x_pre_ready")
        s_mv, s_rstd = sem("moments_ready"), sem("rstd_ready")
        s_z, s_zT, s_zhi, s_zlo = sem("z_ready"), sem("zT_in_bank"), sem("z_hi_ready"), sem("z_lo_ready")
        s_lg, s_lgmax, s_ex = sem("logits_in_bank"), sem("logits_shifted"), sem("router_exp_ready")
        s_gate, s_gT, s_gTs = sem("gates_ready"), sem("gatesT_in_bank"), sem("gatesT_ready")
        s_gdram = sem("gates_in_dram")
        s_w1_in = [sem(f"w1_loaded{p}") for p in range(2)]
        s_w2_in = [sem(f"w2_loaded{p}") for p in range(2)]
        s_gb = [sem(f"gate_broadcast{p}") for p in range(2)]
        s_wT = sem("expert_weightsT_in_banks")
        s_w1s, s_w2hi, s_w2s = sem("w1_split"), sem("w2_hi_ready"), sem("w2_split")
        s_w1h = sem("w1_hi_ready")
        s_lb, s_lbs, s_b1 = sem("w1_lb_ready"), sem("w1_lb_summed"), sem("b1_ready")
        s_h, s_g, s_hhi, s_hlo = sem("hidden_in_bank"), sem("gelu_ready"), sem("h_hi_ready"), sem("h_lo_ready")
        s_used, s_yg, s_acc = sem("hidden_units_used"), sem("y_gated"), sem("acc_ready")
        s_acc0 = sem("acc_cleared")
        s_fT, s_fmv, s_frstd = sem("moe_out_in_bank"), sem("final_moments"), sem("final_rstd")
        s_fin = sem("final_ready")
        s_out = [sem(f"out{b}_stored") for b in range(B)]

        UNITS = B * HC
        PH = 4
        hid_bank = banks[0:PH]
        y_bank = banks[PH:PH + 2]
        w_bank = banks[6:8]
        sa_bank, att_bank, z_bank, lg_bank = banks[2:4], banks[4:6], banks[0:2], banks[6:8]

        class Unit:

            def __init__(self, rounds, r):
                self.rounds, self.r = rounds, r

            def ahead(self, n):
                return Unit(self.rounds, self.r + n)

            @property
            def u(self):
                return self.rounds * (2 * UNITS) + self.r

            @property
            def real(self):
                return not isinstance(self.rounds, int) or 0 <= self.u < E * UNITS

            @property
            def expert(self):
                return self.rounds * 2 + self.r // UNITS

            @property
            def parity(self):
                return (self.r // UNITS) % 2

            @property
            def half(self):
                return self.rounds + self.r // (2 * UNITS)

            @property
            def tile(self):
                return (self.r // HC) % B

            @property
            def chunk(self):
                return self.r % HC

        def hid_bank_of(unit):
            return hid_bank[unit.r % PH]

        W2_LAG = 2
        PREP_AT = 2 * HC

        def expert_units(eng, emit):
            for r in range(-W2_LAG, 0):
                emit(Unit(0, r))
            for r in range(2 * UNITS):
                emit(Unit(0, r))
            rounds = E // 2 - 1
            with eng.Fori(1, rounds) as i:
                for r in range(2 * UNITS):
                    emit(Unit(i, r))
            for r in range(2 * UNITS):
                emit(Unit(rounds, r))

        def has_next(unit):
            return not isinstance(unit.rounds, int) or unit.expert + 1 < E

        @block.sync
        def _(sp):
            for dst, src in ((rows[C_BK:C_BK + H], bkqv[:, 0:D]), (rows[C_BQ:C_BQ + H], bkqv[:, D:2 * D]),
                             (rows[C_LS:C_LS + E], els), (rows[C_LB:C_LB + E], elb), (rows[C_B2:C_B2 + E], b2),
                             (rows[C_B1:C_B1 + E * HC], b1.rearrange("e (c h) -> (e c) h", c=HC)),
                             (rows[C_RLS:C_RLS + 1], rls.unsqueeze(0)), (rows[C_RLB:C_RLB + 1], rlb.unsqueeze(0)),
                             (rows[C_RW:C_RW + E], rw)):
                sp.dma_start(dst, src).then_inc(s_rows_in, 16)
            for b in range(B):
                sp.dma_start(xs[:, b * JT:(b + 1) * JT, :], x[b].rearrange("(j p) d -> p j d", p=P)).then_inc(s_x_in[b], 16)
            for i in range(4):
                if i >= 1:
                    sp.wait_ge(s_fill, J_W + 2 * i)
                sp.dma_start(w_raw[:], wkqv[4 * i:4 * i + 4].rearrange("h d e -> d h e")).then_inc(s_w_in[i], 16)
                if i == 0:
                    with nc.allow_non_contiguous_dma(reason="value weights"):
                        sp.dma_start(wv_raw[:], wkqv[:, :, 2 * D:].rearrange("h d e -> d h e")).then_inc(s_wv_in, 16)
                    sp.dma_start(row1[:, 0:H * DH].rearrange("p (h e) -> p h e", h=H), bkqv[:, 2 * D:].unsqueeze(0)).then_inc(s_misc_in, 16)
                    sp.dma_start(row1[:, H * DH:H * DH + D], bp.unsqueeze(0)).then_inc(s_misc_in, 16)
                    sp.dma_start(row1[:, H * DH + D:], rb.unsqueeze(0)).then_inc(s_misc_in, 16)
                    sp.dma_start(wp_s[:], wp).then_inc(s_wp_in, 16)
                    sp.dma_start(lb_b[:], elb.unsqueeze(0).to_broadcast([P, E, D])).then_inc(s_misc_in, 16)

            def head(rounds, hh):
                h = rounds * 2 + hh
                p = hh % 2
                first = isinstance(rounds, int)
                if first:
                    sp.wait_ge(s_sact, act_done(J_B))
                    sp.wait_ge(s_sdve, dve_done(J_B - 1))
                else:
                    sp.wait_ge(s_t, h * 4 - 4)
                sp.dma_start(m_cur[p][:].bitcast(f32), m_all[:, h, :, :].bitcast(f32)).then_inc(s_m[p], 16)
                if first:
                    sp.wait_ge(s_sdve, dve_done(JOBS - 1))
                else:
                    sp.wait_ge(s_tlo, h * 4 - 4)
                    sp.wait_ge(s_diag, h * 4 - 4)
                sp.dma_start(s_cur[p][:], s_all[:, h, :]).then_inc(s_s[p], 16)
                if first:
                    sp.wait_ge(s_v_all, 1)
                else:
                    sp.wait_ge(s_pv, h * 4 - 4)
                sp.dma_start(v_cur[p][:], v_all[:, h, :, :]).then_inc(s_v[p], 16)

            for hh in range(2):
                head(0, hh)
            with sp.Fori(1, H // 2) as i:
                for hh in range(2):
                    head(i, hh)

            sp.wait_ge(s_o, G)
            sp.wait_ge(s_pv, G)

            def load_weights(e, p):
                sp.dma_start(w1_raw[p][:], w1[e].rearrange("(c h) d -> h c d", c=HC)).then_inc(s_w1_in[p], 16)
                sp.dma_start(w2_raw[p][:], w2[e]).then_inc(s_w2_in[p], 16)

            def load_gates(e, p):
                sp.dma_start(gate_b[p][:], gates_dram[e, :].unsqueeze(0).to_broadcast([P, T])).then_inc(s_gb[p], 16)

            load_weights(0, 0)
            for b in range(B):
                sp.wait_ge(s_gTs, b + 1)
                sp.dma_start(gates_dram[:, b * N:(b + 1) * N], gatesT[:, b * N:(b + 1) * N]).then_inc(s_gdram, 16)
            sp.wait_ge(s_gdram, 16 * B)
            load_gates(0, 0)

            def next_loads(unit):
                if unit.r % UNITS == 0 and has_next(unit):
                    e, p = unit.expert + 1, 1 - unit.parity
                    wait(sp, s_wT, e - 1)
                    wait(sp, s_lb, e - 1)
                    load_weights(e, p)
                    wait(sp, s_yg, (e - 1) * B)
                    load_gates(e, p)

            expert_units(sp, lambda unit: next_loads(unit) if unit.r >= 0 else None)
            for b in range(B):
                sp.wait_ge(s_fin, b + 1)
                sp.dma_start(out[b].rearrange("(j p) d -> p j d", p=P), x_out[:, b % 2, :, :]).then_inc(s_out[b], 16)
            for b in range(B):
                sp.wait_ge(s_out[b], 16)

        @block.gpsimd
        def _(pool):
            done = [0]

            def link(ins):
                done[0] += 1
                ins.then_inc(s_pchain, 1)
                pool.wait_ge(s_pchain, done[0])

            pool.memset(ones[:], 1.0)
            pool.memset(p_bias[:], P_SCALE)
            pool.memset(zero_bias[:], 0.0)
            pool.memset(neg_half[:], -0.5)
            pool.memset(order[:], 1.0)
            pool.memset(future[:], 0.0)
            pool.memset(ident16[:], 0.0)
            link(pool.memset(ident[:], 0.0))
            pool.affine_select(out=ident[:], in_=ident[:], compare_op=ALU.not_equal, fill=1.0, base=0,
                               pattern=[[-1, P]], channel_multiplier=1)
            pool.affine_select(out=ident16[:], in_=ident16[:], compare_op=ALU.not_equal, fill=1.0, base=0,
                               pattern=[[-1, P]], channel_multiplier=1)
            pool.affine_select(out=future[:], in_=future[:], compare_op=ALU.is_ge, fill=MASKED, base=0,
                               pattern=[[-1, P]], channel_multiplier=1)
            pool.affine_select(out=order[:], in_=order[:], compare_op=ALU.is_ge, fill=0.0, base=-1,
                               pattern=[[1, E], [-1, E]], channel_multiplier=0).then_inc(s_const, 1)

            ident_b = ident[:].unsqueeze(1).to_broadcast([P, JT, P])

            def step(k):
                s = k.at(1)
                if s.real:
                    pool.wait_ge(s_exp, s.g + 1)
                    pool.sem_inc(s_seen, 1)
                    for at in (0, 7 * P):
                        stride = 4 * P if at == 0 else P
                        view = p32[:, s.r % 2, at:at + 2 * stride].rearrange("p (a n) -> p a n", a=2)[:, :, 0:P]
                        ins = pool.affine_select(out=view, in_=view, compare_op=ALU.is_ge, fill=0.0, base=0,
                                                 pattern=[[0, 2], [1, P]], channel_multiplier=-1)
                    ins.then_inc(s_mask, 1)
                s = k.at(-1)
                if s.real:
                    q = s.r % 2
                    if s.b == 0:
                        pool.wait_ge(s_s[s.parity], 16 * s.half + 16)
                    pool.wait_ge(s_max, s.g + 1)
                    wait(pool, s_shift, 2 * s.g - 2)
                    c = s_cur[s.parity][:, 1 + s.b * JT:1 + (s.b + 1) * JT]
                    pool.tensor_tensor(row_tot[:, q, :], row_max[:, s.r % 4, :], c, ALU.add).then_inc(s_shift, 1)
                    pool.wait_ge(s_shift, 2 * s.g + 1)
                    pool.tensor_tensor(shift[:, q, :], c, row_tot[:, q, :], ALU.subtract).then_inc(s_shift, 1)
                    pool.wait_ge(s_shift, 2 * s.g + 2)
                    wait(pool, s_sT, s.g - 1)
                    pool.tensor_tensor(diag[q][:], ident_b, shift[:, q, :].unsqueeze(2).to_broadcast([P, JT, P]),
                                       ALU.mult).then_inc(s_diag, 1)

            attention_steps(pool, step)
            pool.wait_ge(s_o, G)
            pool.wait_ge(s_pv, G)
            pool.memset(acc[:], 0.0).then_inc(s_acc0, 1)

            def inv_std(n, moments_sem, out_sem, eps):
                q = n % 2
                pool.wait_ge(moments_sem, n + 1)
                link(pool.tensor_scalar(var_eps[:, q, :], mv[:, q, :, 1], eps, None, ALU.add))
                pool.tensor_tensor(rstd[:, q, :], var_eps[:, q, :], neg_half[:], ALU.pow).then_inc(out_sem, 1)

            for n in range(2 * B):
                inv_std(n, s_mv, s_rstd, EPS_LN if n % 2 == 0 else EPS_MOE)

            def bias_product(e, half, p):
                pool.wait_ge(s_w1_in[p], 16 * half + 16)
                wait(pool, s_lbs, e)
                pool.tensor_tensor(w1_lb[:], w1_raw[p][:], lb_b[:, e, :].unsqueeze(1).to_broadcast([P, HC, D]),
                                   ALU.mult).then_inc(s_lb, 1)

            bias_product(0, 0, 0)

            def unit_step(unit):
                if unit.r < 0:
                    return
                if unit.r % UNITS == HC and has_next(unit):
                    nxt = unit.ahead(UNITS)
                    bias_product(nxt.expert, nxt.half, nxt.parity)
                if unit.chunk == HC - 1:
                    n = unit.expert * B + unit.tile
                    pool.wait_ge(s_yg, n + 1)
                    wait(pool, s_acc, n)
                    cols_ = acc[:, unit.tile * N:(unit.tile + 1) * N]
                    pool.tensor_tensor(cols_, cols_, y_g[:, unit.tile % 2, :], ALU.add).then_inc(s_acc, 1)

            pool.wait_ge(s_acc0, 1)
            expert_units(pool, unit_step)
            for b in range(B):
                inv_std(b, s_fmv, s_frstd, EPS_LN)

        @block.scalar
        def _(act):
            act.wait_ge(s_const, 1)
            for n in range(JOBS):
                if not act_reads[n]:
                    continue
                act.wait_ge(s_fill, n + 1)
                bk = banks[n % 8]
                if n == 0:
                    ins = act.activation(cols[:], bk[:, 0:C_ALL], ACT.Copy)
                elif n < J_W:
                    b = n - J_X
                    ins = act.activation(xt[0][:, b * N:(b + 1) * N], bk, ACT.Copy)
                elif n < J_M:
                    h0 = 4 * ((n - J_W) // 2)
                    ins = act.activation(wkT[:, h0:h0 + 4, 0:D], bk.rearrange("p (a n) -> p a n", a=4), ACT.Copy)
                elif n < J_B:
                    i = n - J_M
                    ins = act.activation(m_all[:, 2 * i:2 * i + 2, 0, :], bk.rearrange("p (a n) -> p a n", a=2)[:, :, 0:D], ACT.Copy)
                else:
                    ins = act.activation(s_all[:, :, 0], bk[:, 0:H], ACT.Copy)
                ins.then_inc(s_sact, 1)
            act.wait_ge(s_v32, NT // 2)
            act.activation(v_all[:, :, :, 0:DH], v32.rearrange("p t (h e) -> p h t e", h=H), ACT.Copy).then_inc(s_v1, 1)

            def step(k):
                s = k.at(1)
                if s.real:
                    act.wait_ge(s_sT, s.g + 1)
                    wait(act, s_lo, s.g - 1)
                    act.activation(p32[:, s.r % 2, :], sT, ACT.Exp, bias=p_bias[:], scale=float(D) ** -0.5).then_inc(s_exp, 1)
                s = k.at(2)
                if s.real:
                    act.wait_ge(s_pv, s.g + 1)
                    act.activation(o_all[:, s.head, s.b, :, :], ps_o[:, 0:JT * VS].rearrange("p (j e) -> p j e", j=JT)[:, :, 0:VW],
                                   ACT.Copy).then_inc(s_o, 1)
                s = k.at(-2)
                if s.real:
                    if s.b == 0:
                        act.wait_ge(s_s[s.parity], 16 * s.half + 16)
                    act.wait_ge(s_t, s.g + 1)
                    wait(act, s_sT, s.g - 3)
                    act.activation(t_s[0][:, s.r % 4, :], ps_t[:], ACT.Identity, bias=s_cur[s.parity][:, 0:1]).then_inc(s_thi, 1)
                s = k.at(1)
                if s.real:
                    act.wait_ge(s_mask, s.g + 1)
                    wait(act, s_pv, s.g - 1)
                    act.activation(p_hi[:, s.r % 2, :], p32[:, s.r % 2, :], ACT.Copy).then_inc(s_hi, 1)

            act.wait_ge(s_v_all, 1)
            attention_steps(act, step)

            for b in range(B):
                q = b % 2
                act.wait_ge(s_saT_ps, b + 1)
                wait(act, s_att, b - 1)
                act.activation(saT[:, q, :], sa_bank[q], ACT.Copy).then_inc(s_saT, 1)
                act.wait_ge(s_zT, b + 1)
                act.activation(xt[0][:, b * N:(b + 1) * N], z_bank[q], ACT.Copy).then_inc(s_zhi, 1)
                act.wait_ge(s_lgmax, b + 1)
                act.activation(probs[:], probs[:], ACT.Exp, bias=zero_bias[:]).then_inc(s_ex, 1)
                act.wait_ge(s_gT, b + 1)
                act.activation(gatesT[:, b * N:(b + 1) * N], lg_bank[1 - q][0:E, :], ACT.Copy).then_inc(s_gTs, 1)

            def w2_hi(e, p):
                act.wait_ge(s_wT, e + 1)
                act.activation(w2_s[p][0][:], w_bank[1].rearrange("p (c n) -> p c n", c=HC), ACT.Copy).then_inc(s_w2hi, 1)

            w2_hi(0, 0)

            def unit_step(unit):
                v = unit.ahead(W2_LAG)
                if v.real:
                    act.wait_ge(s_h, v.u + 1)
                    if v.r % UNITS == 0:
                        act.wait_ge(s_b1, v.expert + 1)
                    wait(act, s_used, v.u - NH + 1)
                    act.activation(h32[:, v.r % NH, :], hid_bank_of(v), ACT.Gelu,
                                   bias=b1_s[v.parity][:, v.chunk:v.chunk + 1]).then_inc(s_g, 1)
                    act.wait_ge(s_g, v.u + 1)
                    act.activation(h_hi[:, v.r % NH, :], h32[:, v.r % NH, :], ACT.Copy).then_inc(s_hhi, 1)
                if unit.r >= 0 and unit.r % UNITS == PREP_AT and has_next(unit):
                    nxt = unit.ahead(UNITS)
                    w2_hi(nxt.expert, nxt.parity)

            expert_units(act, unit_step)

        @block.vector
        def _(dve):
            done = [0]

            def link(ins):
                done[0] += 1
                ins.then_inc(s_vchain, 1)
                dve.wait_ge(s_vchain, done[0])

            dve.wait_ge(s_const, 1)
            link(dve.tensor_copy(onesr[:], ones[:]))
            for n in range(JOBS):
                if not dve_reads[n]:
                    continue
                dve.wait_ge(s_fill, n + 1)
                bk = banks[n % 8]
                if n == 0:
                    dve.wait_ge(s_sact, 1)
                    dve.tensor_copy(wkT[:, :, D], cols[:, C_BK:C_BK + H]).then_inc(s_sdve, 1)
                    link(dve.tensor_tensor(bias_prod[:], cols[:, C_BK:C_BK + H], cols[:, C_BQ:C_BQ + H], ALU.mult))
                    link(dve.tensor_scalar(rwf[:], cols[:, C_RW:C_RW + E], cols[:, C_RLS:C_RLS + 1], None, ALU.mult))
                    dve.tensor_copy(rlb_b[:], cols[:, C_RLB:C_RLB + 1].to_broadcast([P, P]))
                    link(dve.tensor_copy(rw_s[0][:], rwf[:]))
                    link(dve.tensor_tensor(rw_s[1][:], rwf[:], rw_s[0][:].bitcast(f32), ALU.subtract))
                    dve.tensor_copy(rwf[:], cols[:, C_RW:C_RW + E]).then_inc(s_rw, 1)
                elif n < J_W:
                    b = n - J_X
                    dve.wait_ge(s_sact, act_done(n))
                    dve.tensor_tensor(xt[1][:, b * N:(b + 1) * N], bk, xt[0][:, b * N:(b + 1) * N].bitcast(f32),
                                      ALU.subtract).then_inc(s_sdve, 1)
                elif n < J_M:
                    h0 = 4 * ((n - J_W) // 2)
                    dve.tensor_copy(wqT[:, h0:h0 + 4, :], bk.rearrange("p (a n) -> p a n", a=4)).then_inc(s_sdve, 1)
                elif n < J_B:
                    i = n - J_M
                    v = bk.rearrange("p (a n) -> p a n", a=2)
                    dve.wait_ge(s_sact, act_done(n))
                    dve.tensor_copy(vc32[:, H * DH + 2 * i:H * DH + 2 * i + 2], v[:, :, D])
                    dve.tensor_tensor(m_all[:, 2 * i:2 * i + 2, 1, :], v[:, :, 0:D],
                                      m_all[:, 2 * i:2 * i + 2, 0, :].bitcast(f32), ALU.subtract).then_inc(s_sdve, 1)
                elif n == J_B:
                    dve.wait_ge(s_sact, act_done(n))
                    dve.tensor_copy(rbias[:], bk[:, H + VC + D:H + VC + D + E])
                    dve.tensor_copy(vc_bias[:], bk[:, H:H + VC + D]).then_inc(s_sdve, 1)
                    dve.wait_ge(s_wv_in, 16)
                    link(dve.tensor_copy(vc32[:, 0:H * DH], wv_raw[:].rearrange("p h e -> p (h e)")))
                    dve.wait_ge(s_sdve, dve_done(n))
                    link(dve.tensor_copy(vc[0][:], vc32[:]))
                    dve.tensor_tensor(vc[1][:], vc32[:], vc[0][:].bitcast(f32), ALU.subtract).then_inc(s_vcw, 1)
                else:
                    i = n - J_V
                    v = bk.rearrange("p (a n) -> p a n", a=2)
                    dve.tensor_tensor(v32[:, 2 * i:2 * i + 2, :], v[:, :, 0:H * DH],
                                      vc_bias[:, 0:H * DH].unsqueeze(1).to_broadcast([P, 2, H * DH]), ALU.add).then_inc(s_v32, 1)
                    dve.tensor_tensor(s_all[:, :, 1 + 2 * i:3 + 2 * i].rearrange("p h a -> p a h"), v[:, :, H * DH:VC],
                                      vc_bias[:, H * DH:VC].unsqueeze(1).to_broadcast([P, 2, H]), ALU.add).then_inc(s_sdve, 1)
            v4 = v32.rearrange("p t (h e) -> p h t e", h=H)
            dve.wait_ge(s_v1, 1)
            dve.wait_ge(s_sdve, dve_done(JOBS - 1))
            link(dve.tensor_tensor(v4, v4, v_all[:, :, :, 0:DH], ALU.subtract))
            link(dve.tensor_copy(v_all[:, :, :, DH:2 * DH], v4))
            link(dve.tensor_tensor(v_all[:, :, :, 2 * DH:3 * DH], v4, v_all[:, :, :, DH:2 * DH], ALU.subtract))
            link(dve.memset(v_all[:, :, :, 3 * DH:VS], 1.0))
            dve.tensor_tensor(xs[:], xs[:], vc_bias[:, VC:VC + D].unsqueeze(1).to_broadcast([P, NT, D]), ALU.add).then_inc(s_v_all, 1)

            def step(k):
                s = k.at(-1)
                if s.real:
                    dve.wait_ge(s_rowsc, s.g + 1)
                    wait(dve, s_diag, s.g - 3)
                    for j in range(JT):
                        bk, at = R_AT[j]
                        ins = dve.tensor_reduce(row_max[:, s.r % 4, j:j + 1], ps_rows[:, bk, at:at + (j + 1) * P], AX.X, ALU.max)
                    ins.then_inc(s_max, 1)
                s = k.at(-2)
                if s.real:
                    if s.b == 0:
                        dve.wait_ge(s_s[s.parity], 16 * s.half + 16)
                    dve.wait_ge(s_thi, s.g + 1)
                    dve.scalar_tensor_tensor(t_s[1][:, s.r % 4, :], ps_t[:], s_cur[s.parity][:, 0:1], t_s[0][:, s.r % 4, :].bitcast(f32),
                                             op0=ALU.add, op1=ALU.subtract).then_inc(s_tlo, 1)
                s = k.at(1)
                if s.real:
                    dve.wait_ge(s_hi, s.g + 1)
                    wait(dve, s_pv, s.g - 1)
                    dve.tensor_tensor(p_lo[:, s.r % 2, :], p32[:, s.r % 2, :], p_hi[:, s.r % 2, :], ALU.subtract).then_inc(s_lo, 1)

            attention_steps(dve, step)
            dve.wait_ge(s_o, G)
            dve.wait_ge(s_pv, G)

            def moments(q, tiles):
                for j in range(JT):
                    ins = dve.bn_stats(bn6[:, q, j, :], tiles[:, j, :])
                link(ins)
                for j in range(JT):
                    ins = dve.bn_aggr(mv[:, q, j, :], bn6[:, q, j, :])
                return ins

            def normalise(dst, q, tiles):
                for j in range(JT):
                    ins = dve.tensor_scalar(dst[:, j, :], tiles[:, j, :], mv[:, q, j, 0:1], rstd[:, q, j:j + 1],
                                            ALU.subtract, ALU.mult)
                return ins

            for b in range(B):
                q = b % 2
                o = o_all[:, :, b, :, :]
                dve.reciprocal(a_den[:, q], o[:, :, :, 3 * DH])
                link(dve.tensor_tensor(a_num[:, q], o[:, :, :, 0:DH], o[:, :, :, DH:2 * DH], ALU.add))
                link(dve.tensor_tensor(a_num[:, q], a_num[:, q], o[:, :, :, 2 * DH:3 * DH], ALU.add))
                for j in range(JT):
                    ins = dve.tensor_tensor(sa[:, q, j, :].rearrange("p (h e) -> p h e", h=H), a_num[:, q, :, j, :],
                                            a_den[:, q, :, j].unsqueeze(2).to_broadcast([P, H, DH]), ALU.mult)
                ins.then_inc(s_sa, 1)
                dve.wait_ge(s_att, b + 1)
                tiles = xs[:, b * JT:(b + 1) * JT, :]
                link(dve.tensor_tensor(x_pre[:, q], att_bank[q].rearrange("p (j n) -> p j n", j=JT), tiles, ALU.add))
                moments(0, x_pre[:, q]).then_inc(s_mv, 1)
                dve.wait_ge(s_rstd, 2 * b + 1)
                link(normalise(tiles, 0, x_pre[:, q]))
                moments(1, tiles).then_inc(s_mv, 1)
                dve.wait_ge(s_rstd, 2 * b + 2)
                normalise(z[:, q], 1, tiles).then_inc(s_z, 1)
                dve.wait_ge(s_zhi, b + 1)
                dve.tensor_tensor(xt[1][:, b * N:(b + 1) * N], z_bank[q], xt[0][:, b * N:(b + 1) * N].bitcast(f32),
                                  ALU.subtract).then_inc(s_zlo, 1)
                dve.wait_ge(s_lg, b + 1)
                lg = lg_bank[q][:, 0:JT * E].rearrange("p (j e) -> p j e", j=JT)
                link(dve.tensor_tensor(probs[:], lg, rbias[:].unsqueeze(1).to_broadcast([P, JT, E]), ALU.add))
                link(dve.tensor_reduce(top[:], probs[:], AX.X, ALU.max))
                dve.tensor_tensor(probs[:], probs[:], top[:].unsqueeze(2).to_broadcast([P, JT, E]), ALU.subtract).then_inc(s_lgmax, 1)
                dve.wait_ge(s_ex, b + 1)
                link(dve.tensor_reduce(tot[:], probs[:], AX.X, ALU.add))
                link(dve.reciprocal(tot[:], tot[:]))
                link(dve.tensor_tensor(probs[:], probs[:], tot[:].unsqueeze(2).to_broadcast([P, JT, E]), ALU.mult))
                mine = probs[:].unsqueeze(3).to_broadcast([P, JT, E, E])
                other = probs[:].unsqueeze(2).to_broadcast([P, JT, E, E])
                for j in range(JT):
                    dve.tensor_tensor(pair_gt[:, j], other[:, j], mine[:, j], ALU.is_gt)
                    ins = dve.tensor_tensor(pair_eq[:, j], other[:, j], mine[:, j], ALU.is_equal)
                link(ins)
                link(dve.tensor_tensor(pair_eq[:].rearrange("p j a b -> p j (a b)"), pair_eq[:].rearrange("p j a b -> p j (a b)"),
                                       order[:].rearrange("p a b -> p (a b)").unsqueeze(1).to_broadcast([P, JT, E * E]), ALU.mult))
                link(dve.tensor_tensor(pair_gt[:], pair_gt[:], pair_eq[:], ALU.add))
                link(dve.tensor_reduce(rank[:], pair_gt[:], AX.X, ALU.add))
                link(dve.scalar_tensor_tensor(gates[:], rank[:], 1.5, probs[:], op0=ALU.is_lt, op1=ALU.mult))
                link(dve.tensor_reduce(tot[:], gates[:], AX.X, ALU.add))
                link(dve.reciprocal(tot[:], tot[:]))
                dve.tensor_tensor(gates[:], gates[:], tot[:].unsqueeze(2).to_broadcast([P, JT, E]), ALU.mult).then_inc(s_gate, 1)
                dve.wait_ge(s_gT, b + 1)

            def split_weights(e, p):
                dve.wait_ge(s_wT, e + 1)
                ls = cols[:, C_LS:C_LS + E][:, e:e + 1] if isinstance(e, int) else cols[:, C_LS:C_LS + E][:, bass.ds(e, 1)]
                dve.tensor_scalar(w1_s[p][0][:], w_bank[0], ls, None, ALU.mult).then_inc(s_w1h, 1)
                dve.wait_ge(s_w1h, e + 1)
                dve.scalar_tensor_tensor(w1_s[p][1][:], w_bank[0], ls, w1_s[p][0][:].bitcast(f32),
                                         op0=ALU.mult, op1=ALU.subtract).then_inc(s_w1s, 1)
                dve.wait_ge(s_w2hi, e + 1)
                dve.tensor_tensor(w2_s[p][1][:], w_bank[1].rearrange("p (c n) -> p c n", c=HC), w2_s[p][0][:].bitcast(f32),
                                  ALU.subtract).then_inc(s_w2s, 1)
                dve.wait_ge(s_lb, e + 1)
                wait(dve, s_b1, e)
                dve.tensor_reduce(w1_lb_sum[:], w1_lb[:], AX.X, ALU.add).then_inc(s_lbs, 1)
                dve.wait_ge(s_lbs, e + 1)
                b1c = cols[:, C_B1:C_B1 + E * HC].rearrange("p (e c) -> p e c", e=E)[:, e, :]
                dve.tensor_tensor(b1_s[p][:], w1_lb_sum[:], b1c, ALU.add).then_inc(s_b1, 1)

            split_weights(0, 0)

            def unit_step(unit):
                v = unit.ahead(W2_LAG)
                if v.real:
                    dve.wait_ge(s_hhi, v.u + 1)
                    dve.tensor_tensor(h_lo[:, v.r % NH, :], h32[:, v.r % NH, :], h_hi[:, v.r % NH, :].bitcast(f32),
                                      ALU.subtract).then_inc(s_hlo, 1)
                if unit.r < 0:
                    return
                if unit.r % UNITS == PREP_AT and has_next(unit):
                    nxt = unit.ahead(UNITS)
                    split_weights(nxt.expert, nxt.parity)
                if unit.chunk == HC - 1:
                    n = unit.expert * B + unit.tile
                    dve.wait_ge(s_used, (n + 1) * HC)
                    if unit.tile == 0:
                        dve.wait_ge(s_gb[unit.parity], 16 * unit.half + 16)
                    wait(dve, s_acc, n - 1)
                    b2c = cols[:, C_B2:C_B2 + E]
                    b2c = b2c[:, unit.expert:unit.expert + 1] if isinstance(unit.expert, int) else b2c[:, bass.ds(unit.expert, 1)]
                    dve.scalar_tensor_tensor(y_g[:, unit.tile % 2, :], y_bank[unit.tile % 2], b2c,
                                             gate_b[unit.parity][:, unit.tile * N:(unit.tile + 1) * N],
                                             op0=ALU.add, op1=ALU.mult).then_inc(s_yg, 1)

            expert_units(dve, unit_step)
            for b in range(B):
                q = b % 2
                dve.wait_ge(s_fT, b + 1)
                tiles = xs[:, b * JT:(b + 1) * JT, :]
                link(dve.tensor_tensor(x_pre[:, q], hid_bank[q].rearrange("p (j n) -> p j n", j=JT), tiles, ALU.add))
                moments(q, x_pre[:, q]).then_inc(s_fmv, 1)
                dve.wait_ge(s_frstd, b + 1)
                if b >= 2:
                    dve.wait_ge(s_out[b - 2], 16)
                normalise(x_out[:, q], q, x_pre[:, q]).then_inc(s_fin, 1)

        @block.tensor
        def _(pe):
            def three(dst, lhs, rhs, start=True, stop=True):
                pe.matmul(dst, lhs[0], rhs[0], start=start, stop=False)
                pe.matmul(dst, lhs[0], rhs[1], start=False, stop=False)
                return pe.matmul(dst, lhs[1], rhs[0], start=False, stop=stop)

            pe.wait_ge(s_const, 1)
            for n in range(JOBS):
                if n >= 8:
                    pe.wait_ge(s_sact, act_done(n - 8))
                    pe.wait_ge(s_sdve, dve_done(n - 8))
                bk = banks[n % 8]
                if n == 0:
                    pe.wait_ge(s_rows_in, 16 * 9)
                    ins = pe.transpose(bk[:, 0:C_ALL], rows[:], ident[0:C_ALL, 0:C_ALL])
                elif n < J_W:
                    b = n - J_X
                    pe.wait_ge(s_x_in[b], 16)
                    for j in range(JT):
                        ins = pe.transpose(bk[:, j * P:(j + 1) * P], xs[:, b * JT + j, :], ident[:])
                elif n < J_M:
                    i = n - J_W
                    pe.wait_ge(s_w_in[i // 2], 16)
                    for a in range(4):
                        ins = pe.transpose(bk[:, a * D:(a + 1) * D], w_raw[:, a, (i % 2) * D:(i % 2 + 1) * D], ident[:])
                elif n < J_B:
                    i = n - J_M
                    pe.wait_ge(s_sact, act_done(J_W + 2 * (i // 2)))
                    pe.wait_ge(s_sdve, dve_done(J_W + 2 * (i // 2) + 1))
                    for a in range(2):
                        ins = pe.matmul(bk[:, a * 256:a * 256 + D + 1], wqT[:, 2 * i + a, :], wkT[:, 2 * i + a, :], start=True, stop=True)
                elif n == J_B:
                    for h in range(H):
                        pe.matmul(bk[:, h:h + 1], wkT[:, h, 0:D], cols[:, C_BQ + h:C_BQ + h + 1], start=True, stop=True)
                    pe.wait_ge(s_misc_in, 16 * 4)
                    pe.wait_ge(s_rw, 1)
                    pe.matmul(bk[:, H:H + H * DH], ones[0:1, :], row1[:, 0:H * DH], start=True, stop=True)
                    pe.matmul(bk[:, H + H * DH:H + VC], ones[:], bias_prod[:], start=True, stop=True)
                    pe.matmul(bk[:, H + VC:H + VC + D], ones[0:1, :], row1[:, H * DH:H * DH + D], start=True, stop=True)
                    rbk = bk[:, H + VC + D:H + VC + D + E]
                    pe.matmul(rbk, ones[0:1, :], row1[:, H * DH + D:], start=True, stop=False)
                    ins = pe.matmul(rbk, rlb_b[:], rwf[:], start=False, stop=True)
                else:
                    i = n - J_V
                    if i == 0:
                        pe.wait_ge(s_vcw, 1)
                    for a in range(2):
                        t = 2 * i + a
                        ins = three(bk[:, a * 256:a * 256 + VC], [w[:, t * P:(t + 1) * P] for w in xt], [w[:] for w in vc])
                ins.then_inc(s_fill, 1)
            pe.wait_ge(s_sdve, dve_done(JOBS - 1))
            pe.wait_ge(s_sact, act_done(JOBS - 1))

            def step(k):
                s = k.at(-1)
                if s.real:
                    pe.wait_ge(s_thi, s.g + 1)
                    wait(pe, s_max, s.g)
                    for j in range(JT):
                        bk, at = R_AT[j]
                        dst = ps_rows[:, bk, at:at + (j + 1) * P]
                        pe.matmul(dst, t_s[0][:, s.r % 4, j * P:(j + 1) * P], xt[0][:, s.b * N:s.b * N + (j + 1) * P], start=True, stop=False)
                        ins = pe.matmul(ps_rows[:, bk, at + j * P:at + (j + 1) * P], ident16[:], future[:], start=False, stop=True)
                    ins.then_inc(s_rowsc, 1)
                s = k.at(2)
                if s.real:
                    pe.wait_ge(s_lo, s.g + 1)
                    if s.b == 0:
                        pe.wait_ge(s_v[s.parity], 16 * s.half + 16)
                    wait(pe, s_o, s.g)
                    for j in range(JT):
                        for m in range(j + 1):
                            at = T_AT[m] + (j - m) * P
                            for part, src in enumerate((p_hi, p_lo)):
                                ins = pe.matmul(ps_o[:, j * VS:j * VS + VW], src[:, s.r % 2, at:at + P],
                                                v_cur[s.parity][:, s.b * JT + m, 0:VW], start=(m == 0 and part == 0), stop=(m == j and part == 1))
                    ins.then_inc(s_pv, 1)
                s = k.at(-2)
                if s.real:
                    if s.b == 0:
                        pe.wait_ge(s_m[s.parity], 16 * s.half + 16)
                    wait(pe, s_tlo, s.g)
                    three(ps_t[:], [m_cur[s.parity][:, i, :] for i in range(2)], [w[:, s.b * N:(s.b + 1) * N] for w in xt]).then_inc(s_t, 1)
                s = k
                if s.real:
                    pe.wait_ge(s_tlo, s.g + 1)
                    wait(pe, s_exp, s.g)
                    for m in (0, 1, 3, 2):
                        n = (JT - m) * P
                        q0 = m * P
                        three(sT[:, T_AT[m]:T_AT[m] + n], [w[:, s.b * N + q0:s.b * N + q0 + P] for w in xt],
                              [w[:, s.r % 4, q0:N] for w in t_s], stop=False)
                        if m == 0:
                            pe.wait_ge(s_diag, s.g + 1)
                        ins = pe.matmul(sT[:, T_AT[m]:T_AT[m] + n], onesr[:], diag[s.r % 2][:].rearrange("p j n -> p (j n)")[:, q0:N],
                                        start=False, stop=True)
                    ins.then_inc(s_sT, 1)

            attention_steps(pe, step)
            pe.wait_ge(s_wp_in, 16)
            for b in range(B):
                q = b % 2
                pe.wait_ge(s_sa, b + 1)
                for j in range(JT):
                    ins = pe.transpose(sa_bank[q][:, j * P:(j + 1) * P], sa[:, q, j, :], ident[:])
                ins.then_inc(s_saT_ps, 1)
                pe.wait_ge(s_saT, b + 1)
                for j in range(JT):
                    ins = pe.matmul(att_bank[q][:, j * P:(j + 1) * P], saT[:, q, j * P:(j + 1) * P], wp_s[:], start=True, stop=True)
                ins.then_inc(s_att, 1)
                pe.wait_ge(s_z, b + 1)
                for j in range(JT):
                    ins = pe.transpose(z_bank[q][:, j * P:(j + 1) * P], z[:, q, j, :], ident[:])
                ins.then_inc(s_zT, 1)
                pe.wait_ge(s_zlo, b + 1)
                if b >= 1:
                    pe.wait_ge(s_gTs, b)
                for j in range(JT):
                    t = b * JT + j
                    ins = three(lg_bank[q][:, j * E:(j + 1) * E], [w[:, t * P:(t + 1) * P] for w in xt], [w[:] for w in rw_s])
                ins.then_inc(s_lg, 1)
                pe.wait_ge(s_gate, b + 1)
                for j in range(JT):
                    ins = pe.transpose(lg_bank[1 - q][0:E, j * P:(j + 1) * P], gates[:, j, :], ident[:])
                ins.then_inc(s_gT, 1)

            def transpose_weights(e, half, p):
                pe.wait_ge(s_w1_in[p], 16 * half + 16)
                pe.wait_ge(s_w2_in[p], 16 * half + 16)
                wait(pe, s_w1s, e)
                wait(pe, s_w2s, e)
                for c in range(HC):
                    pe.transpose(w_bank[0][:, c * P:(c + 1) * P], w1_raw[p][:, c, :], ident[:])
                for c in range(HC):
                    ins = pe.transpose(w_bank[1][:, c * P:(c + 1) * P], w2_raw[p][:, c * P:(c + 1) * P], ident[:])
                ins.then_inc(s_wT, 1)

            pe.wait_ge(s_gTs, B)
            transpose_weights(0, 0, 0)

            def unit_step(unit):
                v = unit.ahead(W2_LAG)
                if v.real:
                    if v.r % UNITS == 0:
                        pe.wait_ge(s_w1s, v.expert + 1)
                    wait(pe, s_g, v.u - PH + 1)
                    c, t0 = v.chunk, v.tile * N
                    three(hid_bank_of(v), [w[:, c * P:(c + 1) * P] for w in w1_s[v.parity]], [w[:, t0:t0 + N] for w in xt]).then_inc(s_h, 1)
                if unit.r < 0:
                    return
                if unit.r % UNITS == 0:
                    pe.wait_ge(s_w2s, unit.expert + 1)
                pe.wait_ge(s_hlo, unit.u + 1)
                n = unit.expert * B + unit.tile
                if unit.chunk == 0:
                    wait(pe, s_yg, n - 1)
                ins = three(y_bank[unit.tile % 2], [w[:, unit.chunk, :] for w in w2_s[unit.parity]],
                            [w[:, unit.r % NH, :] for w in (h_hi, h_lo)], start=(unit.chunk == 0), stop=(unit.chunk == HC - 1))
                ins.then_inc(s_used, 1)
                if unit.r % UNITS == PREP_AT and has_next(unit):
                    nxt = unit.ahead(UNITS)
                    transpose_weights(nxt.expert, nxt.half, nxt.parity)

            expert_units(pe, unit_step)
            for b in range(B):
                pe.wait_ge(s_acc, (E - 1) * B + b + 1)
                if b >= 2:
                    pe.wait_ge(s_fmv, b - 1)
                for j in range(JT):
                    t = b * JT + j
                    ins = pe.transpose(hid_bank[b % 2][:, j * P:(j + 1) * P], acc[:, t * P:(t + 1) * P], ident[:])
                ins.then_inc(s_fT, 1)


_INS = ["L0_attn_x", "L0_attn_Wkqv", "L0_attn_bkqv", "L0_attn_Wp", "L0_attn_bp", "L0_ffn_router_ln_scale",
        "L0_ffn_router_ln_bias", "L0_ffn_router_w", "L0_ffn_router_b", "L0_ffn_expert_ln_scale",
        "L0_ffn_expert_ln_bias", "L0_ffn_w1", "L0_ffn_b1", "L0_ffn_w2", "L0_ffn_b2"]


def kernel(**inputs):
    import numpy as _np
    import concourse.bacc as _bacc
    from concourse import mybir as _mybir
    from concourse.bass_utils import run_bass_kernel_spmd as _run

    nc = _bacc.Bacc("TRN2", target_bir_lowering=False, num_devices=1)
    arrays, args = {}, []
    for name in _INS:
        a = _np.ascontiguousarray(inputs[name])
        arrays[f"in_{name}"] = a
        args.append(nc.dram_tensor(f"in_{name}", a.shape, _mybir.dt.from_np(a.dtype), kind="ExternalInput").ap())
    args.append(nc.dram_tensor("out", (B, N, D), _mybir.dt.float32, kind="ExternalOutput").ap())
    post_ln_layer(nc, *args)
    r = _run(nc, [arrays], core_ids=[0])
    return r.results[0]["out"]
```

```python
from contextlib import ExitStack

import numpy as np

import concourse.bass as bass
from concourse import mybir

B, N, D = 4, 512, 128
H, DH = 16, 8
E, HID = 8, 512
P = 128
JT = N // P
NT = B * JT
T = B * N
HC = HID // P
G = H * B
BLK = JT * (JT + 1) // 2
SC = BLK * P
VW = 3 * DH + 1
VS = 32
NP = 4
VC = H * DH + H
EPS_LN, EPS_MOE = 1e-5, 1e-6
MASKED = -1e30
P_SCALE = float(np.log(64.0))
T_AT = {0: 0, 1: 4 * P, 3: 7 * P, 2: 8 * P}
R_AT = {3: (0, 0), 2: (1, 0), 0: (1, 3 * P), 1: (2, 0)}

C_BK, C_BQ, C_LS, C_LB, C_B2 = 0, H, 2 * H, 2 * H + E, 2 * H + 2 * E
C_B1 = C_B2 + E
C_RLS = C_B1 + E * HC
C_RLB = C_RLS + 1
C_RW = C_RLB + 1
C_ALL = C_RW + E


class Step:

    def __init__(self, rounds, r):
        self.rounds, self.r = rounds, r

    def at(self, lag):
        return Step(self.rounds, self.r - lag)

    @property
    def g(self):
        return self.rounds * 8 + self.r

    @property
    def real(self):
        return not isinstance(self.rounds, int) or 0 <= self.g < G

    @property
    def b(self):
        return self.r % B

    @property
    def head(self):
        return self.rounds * 2 + self.r // B

    @property
    def half(self):
        return self.rounds + self.r // (2 * B)

    @property
    def parity(self):
        return (self.r // B) % 2


FIRST_STEP, LOOP_STEP, LAST_STEP = -2, 6, G + 3


def attention_steps(eng, emit, after=lambda k: None):
    for k in range(FIRST_STEP, LOOP_STEP):
        emit(Step(0, k))
        after(k)
    rounds = G // 8 - 1
    with eng.Fori(0, rounds) as i:
        for r in range(LOOP_STEP, LOOP_STEP + 8):
            emit(Step(i, r))
    for r in range(LOOP_STEP, LAST_STEP - 8 * rounds + 1):
        emit(Step(rounds, r))
        after(8 * rounds + r)


def wait(eng, sem, value):
    if isinstance(value, int) and value <= 0:
        return
    eng.wait_ge(sem, value)


def post_ln_layer(nc, x, wkqv, bkqv, wp, bp, rls, rlb, rw, rb, els, elb, w1, b1, w2, b2, out):
    f32, f32r = mybir.dt.float32, mybir.dt.float32r
    bf16, f16 = mybir.dt.bfloat16, mybir.dt.float16
    ACT, ALU, AX = mybir.ActivationFunctionType, mybir.AluOpType, mybir.AxisListType

    gates_dram = nc.dram_tensor("gates_by_expert", [E, T], f32, kind="Internal").ap()

    ctx = ExitStack()
    early = ExitStack()
    with ctx:
        def sb(name, shape, dt, stack=ctx):
            return stack.enter_context(nc.sbuf_tensor(name, shape, dt))

        def sem(name):
            return ctx.enter_context(nc.semaphore(name))

        ident = sb("ident", [P, P], f32)
        ident16 = sb("ident16", [P, P], bf16)
        future = sb("future", [P, P], bf16)
        ones = sb("ones", [P, P], f32)
        onesr = sb("onesr", [P, P], f32r)
        p_bias = sb("p_bias", [P, 1], f32)
        neg_half = sb("neg_half", [P, JT], f32)
        order = sb("order", [P, E, E], bf16)
        xs = sb("xs", [P, NT, D], f32)
        xt = [sb("xt_hi", [P, T], f32r), sb("xt_lo", [P, T], f32r)]
        cols = sb("cols", [P, C_ALL], f32)
        rw_s = [sb("rw_hi", [P, E], f32r), sb("rw_lo", [P, E], f32r)]
        rwf = sb("rwf", [P, E], f32)
        rbias = sb("rbias", [P, E], f32)
        rlb_b = sb("rlb_b", [P, P], f32)
        vc_bias = sb("vc_bias", [P, VC + D], f32)
        wp_s = sb("wp_s", [D, D], f32)
        lb_b = sb("lb_b", [P, E, D], f32)
        sa_all = sb("sa_all", [P, NT, D], f32)
        w1_raw = [sb(f"w1_raw{p}", [P, HC, D], f32) for p in range(2)]
        w2_raw = [sb(f"w2_raw{p}", [D, HID], f32) for p in range(2)]
        w1_s = [[sb(f"w1_{n}{p}", [D, HID], f32r) for n in ("hi", "lo")] for p in range(2)]
        w2_s = [[sb(f"w2_{n}{p}", [P, HC, D], f32r) for n in ("hi", "lo")] for p in range(2)]
        w1_lb = sb("w1_lb", [P, HC, D], f32)
        w1_lb_sum = sb("w1_lb_sum", [P, HC], f32)
        b1_s = [sb(f"b1_s{p}", [P, HC], f32) for p in range(2)]

        saT = sb("saT", [P, 2, N], f32)
        x_pre = sb("x_pre", [P, B, JT, D], f32)
        z = sb("z", [P, 2, JT, D], f32)
        bn6 = sb("bn6", [P, 2 * B, JT, 6], f32)
        mv = sb("mv", [P, 2 * B, JT, 2], f32)
        var_eps = sb("var_eps", [P, 2 * B, JT], f32)
        rstd = sb("rstd", [P, 2 * B, JT], f32)
        logits = sb("logits", [P, JT, E], f32)
        kept_logits = sb("kept_logits", [P, JT, E], f32)
        half_sum = sb("half_sum", [P, JT], f32)
        half_kept = sb("half_kept", [P, 2, JT, E], f32)
        margin = sb("margin", [P, 2, JT, E], f32)
        pair_gt = sb("pair_gt", [P, JT, E, E], bf16)
        pair_eq = sb("pair_eq", [P, JT, E, E], bf16)
        rank = sb("rank", [P, JT, E], f32)
        gates = sb("gates", [P, 2, JT, E], f32)
        gatesT = sb("gatesT", [E, T], f32)
        m_all = sb("m_all", [P, H, 2, D], f32r, early)
        v_all = sb("v_all", [P, H, NT, VS], bf16, early)
        s_all = sb("s_all", [P, H, 1 + NT], f32, early)
        m_cur = [sb(f"m_cur{p}", [P, 2, D], f32r, early) for p in range(2)]
        v_cur = [sb(f"v_cur{p}", [P, NT, VS], bf16, early) for p in range(2)]
        s_cur = [sb(f"s_cur{p}", [P, 1 + NT], f32, early) for p in range(2)]
        row_max = sb("row_max", [P, 4, JT], f32, early)
        row_tot = sb("row_tot", [P, 2, JT], f32, early)
        shift = sb("shift", [P, 2, JT], f32, early)
        diag = [sb(f"diag{p}", [P, JT, P], f32r, early) for p in range(2)]
        o_rec = sb("o_rec", [P, 4, JT, VW], f32, early)
        o_inv = sb("o_inv", [P, 4, JT], f32, early)
        o_sum = sb("o_sum", [P, 2, JT, DH], f32, early)
        setup = ExitStack()
        v32 = sb("v32", [P, NT, H * DH], f32, setup)
        w_raw = sb("w_raw", [D, H, 2 * D + DH], f32, setup)
        wkT = sb("wkT", [D, H, D + 1], f32, setup)
        wqT = sb("wqT", [D, H, D], f32, setup)
        rows = sb("rows", [C_ALL, P], f32, setup)
        row1 = sb("row1", [1, H * DH + D + E], f32, setup)
        bias_prod = sb("bias_prod", [P, H], f32, setup)
        vc32 = sb("vc32", [P, VC], f32, setup)
        vc = [sb("vc_hi", [P, VC], f32r, setup), sb("vc_lo", [P, VC], f32r, setup)]
        setup.close()
        p32 = sb("p32", [P, NP, SC], f32, early)
        p_hi = sb("p_hi", [P, NP, SC], f16, early)
        p_lo = sb("p_lo", [P, NP, SC], f16, early)
        t_s = [sb("t_hi", [P, 4, N], f32r, early), sb("t_lo", [P, 4, N], f32r, early)]
        early.close()

        gate_b = [sb(f"gate_b{p}", [P, T], f32) for p in range(2)]
        NH = 4
        h32 = sb("h32", [P, NH, N], f32)
        h_hi = sb("h_hi", [P, NH, N], f32r)
        h_lo = sb("h_lo", [P, NH, N], f32r)
        y_g = sb("y_g", [P, 2, N], f32)
        acc = sb("acc", [P, T], f32)
        x_out = sb("x_out", [P, 2, JT, D], f32)

        bank = [ctx.enter_context(nc.psum_tensor(f"bank{i}", [P, 512], f32)) for i in range(2)]
        ps_rows = ctx.enter_context(nc.psum_tensor("ps_rows", [P, 3, 512], f32))
        ps_sT = ctx.enter_context(nc.psum_tensor("ps_sT", [P, 3, 512], f32))
        ps_t, ps_o = bank
        banks = [ps_t[:, :], ps_o[:, :]] + [ps_rows[:, i, :] for i in range(3)] + [ps_sT[:, i, :] for i in range(3)]
        sT = ps_sT[:].rearrange("p a n -> p (a n)")[:, 0:SC]

        s_const = sem("const_ready")
        s_rows_in = sem("small_rows_loaded")
        s_x_in = [sem(f"x{b}_loaded") for b in range(B)]
        s_w_in = [sem(f"w{i}_loaded") for i in range(4)]
        s_misc_in = sem("row_biases_loaded")
        s_wp_in = sem("wp_loaded")
        s_fill = sem("setup_bank_filled")
        s_sact = sem("setup_bank_read_by_scalar")
        s_sdve = sem("setup_bank_read_by_vector")
        s_vchain = sem("vector_chain")
        s_pchain = sem("pool_chain")
        s_v_all = sem("values_split")
        s_v1 = sem("v1_v2_ready")
        s_v_rest = sem("v_rest_ready")
        s_xbp = sem("x_plus_bp_ready")
        s_vcw = sem("vc_split")
        s_v32 = sem("v32_ready")
        s_rw = sem("router_weights_ready")
        s_m = [sem(f"m_of_head_here{p}") for p in range(2)]
        s_s = [sem(f"constants_of_head_here{p}") for p in range(2)]
        s_v = [sem(f"v_of_head_here{p}") for p in range(2)]
        s_t, s_thi, s_tlo = sem("t_ready"), sem("t_hi_ready"), sem("t_lo_ready")
        s_rowsc, s_max, s_diag = sem("row_scores_ready"), sem("row_max_ready"), sem("diag_ready")
        s_shift = sem("shift_steps")
        s_sT, s_exp, s_mask = sem("scoresT_ready"), sem("exp_ready"), sem("mask_ready")
        s_seen = sem("exp_seen_by_pool")
        s_hi, s_lo, s_pv, s_o = sem("p_hi_ready"), sem("p_lo_ready"), sem("pv_ready"), sem("o_saved")

        block = ctx.enter_context(nc.Block())

        J_X, J_W, J_M, J_B, J_V = 1, 5, 13, 21, 22
        JOBS = J_V + NT // 2
        act_reads = [n < J_V and not (J_W <= n < J_M and (n - J_W) % 2) for n in range(JOBS)]
        dve_reads = [not (J_W <= n < J_M and (n - J_W) % 2 == 0) for n in range(JOBS)]

        def act_done(n):
            return sum(act_reads[:n + 1])

        def dve_done(n):
            return sum(dve_reads[:n + 1])

        s_inv, s_osum, s_sa = sem("o_inverse_ready"), sem("o_sum_steps"), sem("sa_ready")
        s_saT_ps, s_saT = sem("saT_in_bank"), sem("saT_ready")
        s_att, s_xpre = sem("attention_out_in_bank"), sem("x_pre_ready")
        s_mv = [sem(f"moments{n}_ready") for n in range(2 * B)]
        s_rstd = [sem(f"rstd{n}_ready") for n in range(2 * B)]
        s_z, s_zT, s_zhi, s_zlo = sem("z_ready"), sem("zT_in_bank"), sem("z_hi_ready"), sem("z_lo_ready")
        s_lg, s_lgs = sem("logits_in_bank"), sem("logits_ready")
        s_margin, s_tanh = sem("margins_ready"), sem("tanh_ready")
        s_gate, s_gT, s_gTs = sem("gates_ready"), sem("gatesT_in_bank"), sem("gatesT_ready")
        s_gdram = [sem(f"gates{b}_in_dram") for b in range(B)]
        s_w1_in = [sem(f"w1_loaded{p}") for p in range(2)]
        s_w2_in = [sem(f"w2_loaded{p}") for p in range(2)]
        s_gb0 = [sem(f"first_gates_broadcast{b}") for b in range(B)]
        s_gb = [sem(f"gates_broadcast{p}") for p in range(2)]
        s_wT = sem("expert_weightsT_in_banks")
        s_w1s, s_w2hi, s_w2s = sem("w1_split"), sem("w2_hi_ready"), sem("w2_split")
        s_w1h = sem("w1_hi_ready")
        s_lb, s_lbs, s_b1 = sem("w1_lb_ready"), sem("w1_lb_summed"), sem("b1_ready")
        s_h, s_g, s_hhi, s_hlo = sem("hidden_in_bank"), sem("gelu_ready"), sem("h_hi_ready"), sem("h_lo_ready")
        s_used, s_yg, s_acc = sem("hidden_units_used"), sem("y_gated"), sem("acc_ready")
        s_fT, s_fmv, s_frstd = sem("moe_out_in_bank"), sem("final_moments"), sem("final_rstd")
        s_fin = sem("final_ready")
        s_out = [sem(f"out{b}_stored") for b in range(B)]

        UNITS = B * HC
        PH = 2
        hid_bank = banks[0:2]
        mid_bank = banks[2:4]
        w_bank = banks[4:6]
        y_bank = banks[6:8]
        setup_w_bank = banks[6:8]

        AFTER_PE = {64: ["A0"], 65: ["C0", "A1", "C1", "A2"], 66: ["C2", "A3", "C3"]}
        AFTER_ACT = {64: ["A0"], 65: ["A1", "A2"], 66: ["A3"]}
        AFTER_DVE = {66: ["C0", "C1"], 67: ["F0", "C2", "F1", "C3"]}
        AFTER_POOL = {66: ["R0"], 67: ["R1", "S0", "R2", "S1", "R3"]}
        UNIT_PE = {-2: ["G0", "J0"], 2: ["G1", "J1"], 5: ["M0"], 6: ["G2", "J2"], 9: ["M1"], 10: ["G3", "J3"],
                   13: ["M2"], 16: ["M3"]}
        UNIT_ACT = {-2: ["G0"], 2: ["G1"], 4: ["L0"], 5: ["M0"], 6: ["G2"], 8: ["L1"], 9: ["M1"], 10: ["G3"],
                    12: ["L2"], 13: ["M2"], 15: ["L3"], 16: ["M3"]}
        UNIT_DVE = {-2: ["Z0", "G0", "F2", "Z1"], 0: ["J0"], 2: ["G1", "Z2", "F3"], 3: ["L0"], 4: ["J1"], 6: ["G2", "Z3"],
                    7: ["L1"], 8: ["J2"], 10: ["G3"], 11: ["L2"], 12: ["J3"], 14: ["L3"]}
        UNIT_POOL = {-2: ["S2"], 0: ["S3"]}
        mid_order = [x for t in (AFTER_PE, UNIT_PE) for k in sorted(t) for x in t[k]]
        mid_reader = {"A": s_saT, "C": s_xpre, "G": s_zlo, "J": s_lgs, "M": s_gTs}

        class Unit:

            def __init__(self, rounds, r):
                self.rounds, self.r = rounds, r

            def ahead(self, n):
                return Unit(self.rounds, self.r + n)

            @property
            def u(self):
                return self.rounds * (2 * UNITS) + self.r

            @property
            def real(self):
                return not isinstance(self.rounds, int) or 0 <= self.u < E * UNITS

            @property
            def expert(self):
                return self.rounds * 2 + self.r // UNITS

            @property
            def parity(self):
                return (self.r // UNITS) % 2

            @property
            def half(self):
                return self.rounds + self.r // (2 * UNITS)

            @property
            def tile(self):
                return (self.r // HC) % B

            @property
            def chunk(self):
                return self.r % HC

        def hid_bank_of(unit):
            return hid_bank[unit.r % PH]

        W2_LAG = 2
        PREP_PE, PREP_W1HI, PREP_W1LO, PREP_W2HI, PREP_W2LO, PREP_B1 = 3, 4, 5, 5, 6, 7

        def expert_units(eng, emit):
            for r in range(-W2_LAG, 0):
                emit(Unit(0, r))
            for r in range(2 * UNITS):
                emit(Unit(0, r))
            rounds = E // 2 - 1
            with eng.Fori(1, rounds) as i:
                for r in range(2 * UNITS):
                    emit(Unit(i, r))
            for r in range(2 * UNITS):
                emit(Unit(rounds, r))

        def has_next(unit, n=1):
            return not isinstance(unit.rounds, int) or unit.expert + n < E

        def is_first(unit):
            return isinstance(unit.rounds, int) and unit.expert == 0

        def bank_of(name):
            return mid_bank[mid_order.index(name) % 2]

        def tiles_of(bk):
            return bk.rearrange("p (j n) -> p j n", j=JT)

        @block.sync
        def _(sp):
            for b in range(B):
                sp.dma_start(xs[:, b * JT:(b + 1) * JT, :], x[b].rearrange("(j p) d -> p j d", p=P)).then_inc(s_x_in[b], 16)
            for dst, src in ((rows[C_BK:C_BK + H], bkqv[:, 0:D]), (rows[C_BQ:C_BQ + H], bkqv[:, D:2 * D]),
                             (rows[C_LS:C_LS + E], els), (rows[C_LB:C_LB + E], elb), (rows[C_B2:C_B2 + E], b2),
                             (rows[C_B1:C_B1 + E * HC], b1.rearrange("e (c h) -> (e c) h", c=HC)),
                             (rows[C_RLS:C_RLS + 1], rls.unsqueeze(0)), (rows[C_RLB:C_RLB + 1], rlb.unsqueeze(0)),
                             (rows[C_RW:C_RW + E], rw)):
                sp.dma_start(dst, src).then_inc(s_rows_in, 16)
            sp.dma_start(row1[:, 0:H * DH].rearrange("p (h e) -> p h e", h=H), bkqv[:, 2 * D:].unsqueeze(0)).then_inc(s_misc_in, 16)
            sp.dma_start(row1[:, H * DH:H * DH + D], bp.unsqueeze(0)).then_inc(s_misc_in, 16)
            sp.dma_start(row1[:, H * DH + D:], rb.unsqueeze(0)).then_inc(s_misc_in, 16)
            sp.dma_start(wp_s[:], wp).then_inc(s_wp_in, 16)
            sp.dma_start(lb_b[:], elb.unsqueeze(0).to_broadcast([P, E, D])).then_inc(s_misc_in, 16)

            def load_weights(e, p):
                sp.dma_start(w1_raw[p][:], w1[e].rearrange("(c h) d -> h c d", c=HC)).then_inc(s_w1_in[p], 16)
                sp.dma_start(w2_raw[p][:], w2[e]).then_inc(s_w2_in[p], 16)

            load_weights(0, 0)
            load_weights(1, 1)

            def head(rounds, hh):
                h = rounds * 2 + hh
                p = hh % 2
                first = isinstance(rounds, int)
                if first:
                    sp.wait_ge(s_sact, act_done(J_B))
                    sp.wait_ge(s_sdve, dve_done(J_B - 1))
                else:
                    sp.wait_ge(s_t, h * 4 - 4)
                sp.dma_start(m_cur[p][:].bitcast(f32), m_all[:, h, :, :].bitcast(f32)).then_inc(s_m[p], 16)
                if first:
                    sp.wait_ge(s_sdve, dve_done(JOBS - 1))
                else:
                    sp.wait_ge(s_tlo, h * 4 - 4)
                    sp.wait_ge(s_diag, h * 4 - 4)
                sp.dma_start(s_cur[p][:], s_all[:, h, :]).then_inc(s_s[p], 16)

            def head_values(rounds, hh):
                h = rounds * 2 + hh
                p = hh % 2
                if isinstance(rounds, int):
                    sp.wait_ge(s_v_all, 1)
                else:
                    sp.wait_ge(s_pv, h * 4 - 4)
                sp.dma_start(v_cur[p][:], v_all[:, h, :, :]).then_inc(s_v[p], 16)

            for hh in range(2):
                head(0, hh)
            for hh in range(2):
                head_values(0, hh)
            with sp.Fori(1, H // 2) as i:
                for hh in range(2):
                    head(i, hh)
                    head_values(i, hh)

            def load_gates(e, p):
                sp.dma_start(gate_b[p][:], gates_dram[e, :].unsqueeze(0).to_broadcast([P, T])).then_inc(s_gb[p], 16)

            sp.wait_ge(s_o, G)
            for b in range(B):
                t0 = b * N
                sp.wait_ge(s_gTs, b + 1)
                sp.dma_start(gates_dram[:, t0:t0 + N], gatesT[:, t0:t0 + N]).then_inc(s_gdram[b], 16)
                sp.wait_ge(s_gdram[b], 16)
                sp.dma_start(gate_b[0][:, t0:t0 + N], gates_dram[0, t0:t0 + N].unsqueeze(0).to_broadcast([P, N])).then_inc(s_gb0[b], 16)

            def next_loads(unit):
                if unit.r % UNITS == 0 and has_next(unit):
                    e = unit.expert + 1
                    wait(sp, s_acc, (e - 1) * B)
                    load_gates(e, 1 - unit.parity)
                if unit.r % UNITS == 2 * HC and has_next(unit, 2):
                    sp.wait_ge(s_wT, unit.expert + 1)
                    sp.wait_ge(s_lb, unit.expert + 1)
                    load_weights(unit.expert + 2, unit.parity)

            expert_units(sp, lambda unit: next_loads(unit) if unit.r >= 0 else None)
            for b in range(B):
                sp.wait_ge(s_fin, b + 1)
                sp.dma_start(out[b].rearrange("(j p) d -> p j d", p=P), x_out[:, b % 2, :, :]).then_inc(s_out[b], 16)
            for b in range(B):
                sp.wait_ge(s_out[b], 16)

        @block.gpsimd
        def _(pool):
            done = [0]

            def link(ins):
                done[0] += 1
                ins.then_inc(s_pchain, 1)
                pool.wait_ge(s_pchain, done[0])

            pool.memset(ones[:], 1.0)
            pool.memset(p_bias[:], P_SCALE)
            pool.memset(neg_half[:], -0.5)
            pool.memset(order[:], 1.0)
            pool.memset(future[:], 0.0)
            pool.memset(ident16[:], 0.0)
            link(pool.memset(ident[:], 0.0))
            pool.affine_select(out=ident[:], in_=ident[:], compare_op=ALU.not_equal, fill=1.0, base=0,
                               pattern=[[-1, P]], channel_multiplier=1)
            pool.affine_select(out=ident16[:], in_=ident16[:], compare_op=ALU.not_equal, fill=1.0, base=0,
                               pattern=[[-1, P]], channel_multiplier=1)
            pool.affine_select(out=future[:], in_=future[:], compare_op=ALU.is_ge, fill=MASKED, base=0,
                               pattern=[[-1, P]], channel_multiplier=1)
            pool.affine_select(out=order[:], in_=order[:], compare_op=ALU.is_ge, fill=0.0, base=-1,
                               pattern=[[1, E], [-1, E]], channel_multiplier=0).then_inc(s_const, 1)

            ident_b = ident[:].unsqueeze(1).to_broadcast([P, JT, P])

            v4 = v32[:].rearrange("p t (h e) -> p h t e", h=H)

            def subtract_v1():
                pool.wait_ge(s_v1, 1)
                for h0 in range(0, H, 4):
                    hs = slice(h0, h0 + 4)
                    ins = pool.tensor_tensor(v4[:, hs], v4[:, hs], v_all[:, hs, :, 0:DH], ALU.subtract)
                ins.then_inc(s_v_rest, 1)

            def bias_product(e, half, p):
                pool.wait_ge(s_w1_in[p], 16 * half + 16)
                wait(pool, s_lbs, e)
                pool.tensor_tensor(w1_lb[:], w1_raw[p][:], lb_b[:, e, :].unsqueeze(1).to_broadcast([P, HC, D]),
                                   ALU.mult).then_inc(s_lb, 1)

            def step(k):
                s = k.at(1)
                if s.real:
                    pool.wait_ge(s_exp, s.g + 1)
                    pool.sem_inc(s_seen, 1)
                    for at in (0, 7 * P):
                        stride = 4 * P if at == 0 else P
                        view = p32[:, s.r % NP, at:at + 2 * stride].rearrange("p (a n) -> p a n", a=2)[:, :, 0:P]
                        ins = pool.affine_select(out=view, in_=view, compare_op=ALU.is_ge, fill=0.0, base=0,
                                                 pattern=[[0, 2], [1, P]], channel_multiplier=-1)
                    ins.then_inc(s_mask, 1)
                s = k.at(-1)
                if s.real:
                    q = s.r % 2
                    if s.b == 0:
                        pool.wait_ge(s_s[s.parity], 16 * s.half + 16)
                    pool.wait_ge(s_max, s.g + 1)
                    wait(pool, s_shift, 2 * s.g - 2)
                    c = s_cur[s.parity][:, 1 + s.b * JT:1 + (s.b + 1) * JT]
                    pool.tensor_tensor(row_tot[:, q, :], row_max[:, s.r % 4, :], c, ALU.add).then_inc(s_shift, 1)
                    pool.wait_ge(s_shift, 2 * s.g + 1)
                    pool.tensor_tensor(shift[:, q, :], c, row_tot[:, q, :], ALU.subtract).then_inc(s_shift, 1)
                    pool.wait_ge(s_shift, 2 * s.g + 2)
                    wait(pool, s_sT, s.g - 1)
                    pool.tensor_tensor(diag[q][:], ident_b, shift[:, q, :].unsqueeze(2).to_broadcast([P, JT, P]),
                                       ALU.mult).then_inc(s_diag, 1)

            def heads_output(k):
                s = k.at(4)
                if s.real:
                    q = s.r % 4
                    pool.wait_ge(s_inv, s.g + 1)
                    pool.tensor_tensor(o_sum[:, q % 2], o_rec[:, q, :, 0:DH], o_rec[:, q, :, DH:2 * DH], ALU.add).then_inc(s_osum, 1)
                    pool.wait_ge(s_osum, 2 * s.g + 1)
                    pool.tensor_tensor(o_sum[:, q % 2], o_sum[:, q % 2], o_rec[:, q, :, 2 * DH:3 * DH], ALU.add).then_inc(s_osum, 1)
                    pool.wait_ge(s_osum, 2 * s.g + 2)
                    dst = sa_all[:, s.b * JT:(s.b + 1) * JT, :].rearrange("p j (h e) -> p j h e", h=H)[:, :, s.head, :]
                    pool.tensor_tensor(dst, o_sum[:, q % 2], o_inv[:, q].unsqueeze(2).to_broadcast([P, JT, DH]), ALU.mult).then_inc(s_sa, 1)

            mid = {
                "R": lambda b: inv_std(2 * b, EPS_LN),
                "S": lambda b: inv_std(2 * b + 1, EPS_MOE),
            }

            def inv_std(n, eps):
                pool.wait_ge(s_mv[n], 1)
                link(pool.tensor_scalar(var_eps[:, n, :], mv[:, n, :, 1], eps, None, ALU.add))
                pool.tensor_tensor(rstd[:, n, :], var_eps[:, n, :], neg_half[:], ALU.pow).then_inc(s_rstd[n], 1)

            def full_step(k):
                step(k)
                heads_output(k)

            def after(k):
                if k == -1:
                    pool.wait_ge(s_misc_in, 16 * 4)
                    bias_product(0, 0, 0)
                if k == 3:
                    pool.wait_ge(s_sdve, dve_done(JOBS - 1))
                    pool.tensor_tensor(xs[:], xs[:], vc_bias[:, VC:VC + D].unsqueeze(1).to_broadcast([P, NT, D]), ALU.add).then_inc(s_xbp, 1)
                for name in AFTER_POOL.get(k, []):
                    mid[name[0]](int(name[1]))

            subtract_v1()
            attention_steps(pool, full_step, after)

            def unit_step(unit):
                if isinstance(unit.rounds, int) and unit.rounds == 0:
                    for name in UNIT_POOL.get(unit.r, []):
                        mid[name[0]](int(name[1]))
                if unit.r < 0:
                    return
                if unit.r % UNITS == 2 and has_next(unit):
                    nxt = unit.ahead(UNITS)
                    bias_product(nxt.expert, nxt.half, nxt.parity)
                if unit.chunk == HC - 1:
                    n = unit.expert * B + unit.tile
                    pool.wait_ge(s_yg, n + 1)
                    wait(pool, s_acc, n)
                    tokens = slice(unit.tile * N, (unit.tile + 1) * N)
                    if is_first(unit):
                        pool.wait_ge(s_gb0[unit.tile], 16)
                        pool.tensor_tensor(acc[:, tokens], acc[:, tokens], gate_b[0][:, tokens], ALU.mult).then_inc(s_acc, 1)
                    else:
                        pool.tensor_tensor(acc[:, tokens], acc[:, tokens], y_g[:, unit.tile % 2, :], ALU.add).then_inc(s_acc, 1)

            expert_units(pool, unit_step)
            for b in range(B):
                pool.wait_ge(s_fmv, b + 1)
                link(pool.tensor_scalar(var_eps[:, b, :], mv[:, b, :, 1], EPS_LN, None, ALU.add))
                pool.tensor_tensor(rstd[:, b, :], var_eps[:, b, :], neg_half[:], ALU.pow).then_inc(s_frstd, 1)

        @block.scalar
        def _(act):
            for i in range(4):
                act.dma_start(w_raw[:, 4 * i:4 * i + 4, :], wkqv[4 * i:4 * i + 4].rearrange("h d e -> d h e")).then_inc(s_w_in[i], 16)
            act.wait_ge(s_const, 1)
            for n in range(JOBS):
                if not act_reads[n]:
                    continue
                act.wait_ge(s_fill, n + 1)
                bk = banks[n % 8]
                if n == 0:
                    ins = act.activation(cols[:], bk[:, 0:C_ALL], ACT.Copy)
                elif n < J_W:
                    b = n - J_X
                    ins = act.activation(xt[0][:, b * N:(b + 1) * N], bk, ACT.Copy)
                elif n < J_M:
                    h0 = 4 * ((n - J_W) // 2)
                    ins = act.activation(wkT[:, h0:h0 + 4, 0:D], bk.rearrange("p (a n) -> p a n", a=4), ACT.Copy)
                elif n < J_B:
                    i = n - J_M
                    ins = act.activation(m_all[:, 2 * i:2 * i + 2, 0, :], bk.rearrange("p (a n) -> p a n", a=2)[:, :, 0:D], ACT.Copy)
                else:
                    ins = act.activation(s_all[:, :, 0], bk[:, 0:H], ACT.Copy)
                ins.then_inc(s_sact, 1)
            v4 = v32[:].rearrange("p t (h e) -> p h t e", h=H)
            act.wait_ge(s_v32, NT // 2)
            act.activation(v_all[:, :, :, 0:DH], v4, ACT.Copy).then_inc(s_v1, 1)

            def step(k):
                s = k.at(1)
                if s.real:
                    act.wait_ge(s_sT, s.g + 1)
                    wait(act, s_lo, s.g - NP + 1)
                    act.activation(p32[:, s.r % NP, :], sT, ACT.Exp, bias=p_bias[:], scale=float(D) ** -0.5).then_inc(s_exp, 1)
                s = k.at(3)
                if s.real:
                    act.wait_ge(s_pv, s.g + 1)
                    wait(act, s_sa, s.g - 2)
                    act.activation(o_rec[:, s.r % 4], ps_o[:, 0:JT * VS].rearrange("p (j e) -> p j e", j=JT)[:, :, 0:VW],
                                   ACT.Copy).then_inc(s_o, 1)
                s = k.at(-2)
                if s.real:
                    if s.b == 0:
                        act.wait_ge(s_s[s.parity], 16 * s.half + 16)
                    act.wait_ge(s_t, s.g + 1)
                    wait(act, s_sT, s.g - 3)
                    act.activation(t_s[0][:, s.r % 4, :], ps_t[:], ACT.Identity, bias=s_cur[s.parity][:, 0:1]).then_inc(s_thi, 1)
                s = k.at(1)
                if s.real:
                    act.wait_ge(s_mask, s.g + 1)
                    wait(act, s_pv, s.g - NP + 1)
                    act.activation(p_hi[:, s.r % NP, :], p32[:, s.r % NP, :], ACT.Copy).then_inc(s_hi, 1)

            def w2_hi(e, p, banks_w=w_bank):
                act.wait_ge(s_wT, e + 1)
                act.activation(w2_s[p][0][:], banks_w[1].rearrange("p (c n) -> p c n", c=HC), ACT.Copy).then_inc(s_w2hi, 1)

            def copy_saT(b):
                act.wait_ge(s_saT_ps, b + 1)
                wait(act, s_att, b - 1)
                act.activation(saT[:, b % 2, :], bank_of(f"A{b}"), ACT.Copy).then_inc(s_saT, 1)

            def z_hi(b):
                act.wait_ge(s_zT, b + 1)
                act.activation(xt[0][:, b * N:(b + 1) * N], bank_of(f"G{b}"), ACT.Copy).then_inc(s_zhi, 1)

            def tanh_of_margins(b):
                act.wait_ge(s_margin, b + 1)
                act.activation(margin[:, b % 2], margin[:, b % 2], ACT.Tanh).then_inc(s_tanh, 1)

            def copy_gatesT(b):
                act.wait_ge(s_gT, b + 1)
                act.activation(gatesT[:, b * N:(b + 1) * N], bank_of(f"M{b}")[0:E, :], ACT.Copy).then_inc(s_gTs, 1)

            mid = {"A": copy_saT, "G": z_hi, "L": tanh_of_margins, "M": copy_gatesT}

            def after(k):
                if k == -2:
                    w2_hi(0, 0, setup_w_bank)
                if k == -1:
                    act.wait_ge(s_v_rest, 1)
                    act.activation(v_all[:, :, :, DH:2 * DH], v4, ACT.Copy).then_inc(s_v1, 1)
                if k == 0:
                    act.wait_ge(s_v_all, 1)
                for name in AFTER_ACT.get(k, []):
                    mid[name[0]](int(name[1]))

            attention_steps(act, step, after)

            def unit_step(unit):
                if isinstance(unit.rounds, int) and unit.rounds == 0:
                    for name in UNIT_ACT.get(unit.r, []):
                        mid[name[0]](int(name[1]))
                v = unit.ahead(W2_LAG)
                if v.real:
                    act.wait_ge(s_h, v.u + 1)
                    if v.r % UNITS == 0:
                        act.wait_ge(s_b1, v.expert + 1)
                    wait(act, s_used, v.u - NH + 1)
                    act.activation(h32[:, v.r % NH, :], hid_bank_of(v), ACT.Gelu,
                                   bias=b1_s[v.parity][:, v.chunk:v.chunk + 1]).then_inc(s_g, 1)
                    act.wait_ge(s_g, v.u + 1)
                    act.activation(h_hi[:, v.r % NH, :], h32[:, v.r % NH, :], ACT.Copy).then_inc(s_hhi, 1)
                if unit.r >= 0 and unit.r % UNITS == PREP_W2HI and has_next(unit):
                    nxt = unit.ahead(UNITS)
                    w2_hi(nxt.expert, nxt.parity)

            expert_units(act, unit_step)

        @block.vector
        def _(dve):
            done = [0]

            def link(ins):
                done[0] += 1
                ins.then_inc(s_vchain, 1)
                dve.wait_ge(s_vchain, done[0])

            dve.wait_ge(s_const, 1)
            link(dve.tensor_copy(onesr[:], ones[:]))
            dve.memset(v_all[:, :, :, 3 * DH:VS], 1.0)
            for n in range(JOBS):
                if not dve_reads[n]:
                    continue
                dve.wait_ge(s_fill, n + 1)
                bk = banks[n % 8]
                if n == 0:
                    dve.wait_ge(s_sact, 1)
                    dve.tensor_copy(wkT[:, :, D], cols[:, C_BK:C_BK + H]).then_inc(s_sdve, 1)
                    link(dve.tensor_tensor(bias_prod[:], cols[:, C_BK:C_BK + H], cols[:, C_BQ:C_BQ + H], ALU.mult))
                    link(dve.tensor_scalar(rwf[:], cols[:, C_RW:C_RW + E], cols[:, C_RLS:C_RLS + 1], None, ALU.mult))
                    dve.tensor_copy(rlb_b[:], cols[:, C_RLB:C_RLB + 1].to_broadcast([P, P]))
                    link(dve.tensor_copy(rw_s[0][:], rwf[:]))
                    link(dve.tensor_tensor(rw_s[1][:], rwf[:], rw_s[0][:].bitcast(f32), ALU.subtract))
                    dve.tensor_copy(rwf[:], cols[:, C_RW:C_RW + E]).then_inc(s_rw, 1)
                elif n < J_W:
                    b = n - J_X
                    dve.wait_ge(s_sact, act_done(n))
                    dve.tensor_tensor(xt[1][:, b * N:(b + 1) * N], bk, xt[0][:, b * N:(b + 1) * N].bitcast(f32),
                                      ALU.subtract).then_inc(s_sdve, 1)
                elif n < J_M:
                    h0 = 4 * ((n - J_W) // 2)
                    dve.tensor_copy(wqT[:, h0:h0 + 4, :], bk.rearrange("p (a n) -> p a n", a=4)).then_inc(s_sdve, 1)
                elif n < J_B:
                    i = n - J_M
                    v = bk.rearrange("p (a n) -> p a n", a=2)
                    dve.wait_ge(s_sact, act_done(n))
                    dve.tensor_copy(vc32[:, H * DH + 2 * i:H * DH + 2 * i + 2], v[:, :, D])
                    dve.tensor_tensor(m_all[:, 2 * i:2 * i + 2, 1, :], v[:, :, 0:D],
                                      m_all[:, 2 * i:2 * i + 2, 0, :].bitcast(f32), ALU.subtract).then_inc(s_sdve, 1)
                elif n == J_B:
                    dve.wait_ge(s_sact, act_done(n))
                    dve.tensor_copy(rbias[:], bk[:, H + VC + D:H + VC + D + E])
                    dve.tensor_copy(vc_bias[:], bk[:, H:H + VC + D]).then_inc(s_sdve, 1)
                    for i in range(4):
                        dve.wait_ge(s_w_in[i], 16)
                    link(dve.tensor_copy(vc32[:, 0:H * DH].rearrange("p (h e) -> p h e", h=H), w_raw[:, :, 2 * D:]))
                    dve.wait_ge(s_sdve, dve_done(n))
                    link(dve.tensor_copy(vc[0][:], vc32[:]))
                    dve.tensor_tensor(vc[1][:], vc32[:], vc[0][:].bitcast(f32), ALU.subtract).then_inc(s_vcw, 1)
                else:
                    i = n - J_V
                    v = bk.rearrange("p (a n) -> p a n", a=2)
                    dve.tensor_tensor(v32[:, 2 * i:2 * i + 2, :], v[:, :, 0:H * DH],
                                      vc_bias[:, 0:H * DH].unsqueeze(1).to_broadcast([P, 2, H * DH]), ALU.add).then_inc(s_v32, 1)
                    dve.tensor_tensor(s_all[:, :, 1 + 2 * i:3 + 2 * i].rearrange("p h a -> p a h"), v[:, :, H * DH:VC],
                                      vc_bias[:, H * DH:VC].unsqueeze(1).to_broadcast([P, 2, H]), ALU.add).then_inc(s_sdve, 1)
            def step(k):
                s = k.at(-1)
                if s.real:
                    dve.wait_ge(s_rowsc, s.g + 1)
                    wait(dve, s_diag, s.g - 3)
                    for j in range(JT):
                        bk, at = R_AT[j]
                        ins = dve.tensor_reduce(row_max[:, s.r % 4, j:j + 1], ps_rows[:, bk, at:at + (j + 1) * P], AX.X, ALU.max)
                    ins.then_inc(s_max, 1)
                s = k.at(-2)
                if s.real:
                    if s.b == 0:
                        dve.wait_ge(s_s[s.parity], 16 * s.half + 16)
                    dve.wait_ge(s_thi, s.g + 1)
                    dve.scalar_tensor_tensor(t_s[1][:, s.r % 4, :], ps_t[:], s_cur[s.parity][:, 0:1], t_s[0][:, s.r % 4, :].bitcast(f32),
                                             op0=ALU.add, op1=ALU.subtract).then_inc(s_tlo, 1)
                s = k.at(4)
                if s.real:
                    dve.wait_ge(s_o, s.g + 1)
                    dve.reciprocal(o_inv[:, s.r % 4], o_rec[:, s.r % 4, :, 3 * DH]).then_inc(s_inv, 1)
                s = k.at(1)
                if s.real:
                    dve.wait_ge(s_hi, s.g + 1)
                    wait(dve, s_pv, s.g - NP + 1)
                    dve.tensor_tensor(p_lo[:, s.r % NP, :], p32[:, s.r % NP, :], p_hi[:, s.r % NP, :], ALU.subtract).then_inc(s_lo, 1)

            def moments(n, tiles):
                for j in range(JT):
                    ins = dve.bn_stats(bn6[:, n, j, :], tiles[:, j, :])
                link(ins)
                for j in range(JT):
                    ins = dve.bn_aggr(mv[:, n, j, :], bn6[:, n, j, :])
                return ins

            def normalise(dst, n, tiles):
                for j in range(JT):
                    ins = dve.tensor_scalar(dst[:, j, :], tiles[:, j, :], mv[:, n, j, 0:1], rstd[:, n, j:j + 1],
                                            ALU.subtract, ALU.mult)
                return ins

            def residual(b):
                dve.wait_ge(s_att, b + 1)
                dve.wait_ge(s_xbp, 1)
                dve.tensor_tensor(x_pre[:, b], tiles_of(bank_of(f"C{b}")), xs[:, b * JT:(b + 1) * JT, :], ALU.add).then_inc(s_xpre, 1)
                dve.wait_ge(s_xpre, b + 1)
                moments(2 * b, x_pre[:, b]).then_inc(s_mv[2 * b], 1)

            def first_norm(b):
                dve.wait_ge(s_rstd[2 * b], 1)
                tiles = xs[:, b * JT:(b + 1) * JT, :]
                link(normalise(tiles, 2 * b, x_pre[:, b]))
                moments(2 * b + 1, tiles).then_inc(s_mv[2 * b + 1], 1)

            def experts_norm(b):
                dve.wait_ge(s_rstd[2 * b + 1], 1)
                wait(dve, s_zT, b - 1)
                normalise(z[:, b % 2], 2 * b + 1, xs[:, b * JT:(b + 1) * JT, :]).then_inc(s_z, 1)

            def z_lo(b):
                dve.wait_ge(s_zhi, b + 1)
                dve.tensor_tensor(xt[1][:, b * N:(b + 1) * N], bank_of(f"G{b}"), xt[0][:, b * N:(b + 1) * N].bitcast(f32),
                                  ALU.subtract).then_inc(s_zlo, 1)

            def choose_experts(b):
                dve.wait_ge(s_lg, b + 1)
                lg = bank_of(f"J{b}")[:, 0:JT * E].rearrange("p (j e) -> p j e", j=JT)
                dve.tensor_tensor(logits[:], lg, rbias[:].unsqueeze(1).to_broadcast([P, JT, E]), ALU.add).then_inc(s_lgs, 1)
                dve.wait_ge(s_lgs, b + 1)
                mine = logits[:].unsqueeze(3).to_broadcast([P, JT, E, E])
                other = logits[:].unsqueeze(2).to_broadcast([P, JT, E, E])
                for j in range(JT):
                    dve.tensor_tensor(pair_gt[:, j], other[:, j], mine[:, j], ALU.is_gt)
                    ins = dve.tensor_tensor(pair_eq[:, j], other[:, j], mine[:, j], ALU.is_equal)
                link(ins)
                link(dve.tensor_tensor(pair_eq[:].rearrange("p j a b -> p j (a b)"), pair_eq[:].rearrange("p j a b -> p j (a b)"),
                                       order[:].rearrange("p a b -> p (a b)").unsqueeze(1).to_broadcast([P, JT, E * E]), ALU.mult))
                link(dve.tensor_tensor(pair_gt[:], pair_gt[:], pair_eq[:], ALU.add))
                link(dve.tensor_reduce(rank[:], pair_gt[:], AX.X, ALU.add))
                half = half_kept[:, b % 2]
                link(dve.tensor_scalar(half, rank[:], 1.5, 0.5, ALU.is_lt, ALU.mult))
                link(dve.tensor_tensor(kept_logits[:], half, logits[:], ALU.mult))
                link(dve.tensor_reduce(half_sum[:], kept_logits[:], AX.X, ALU.add))
                dve.tensor_tensor(margin[:, b % 2], logits[:], half_sum[:].unsqueeze(2).to_broadcast([P, JT, E]),
                                  ALU.subtract).then_inc(s_margin, 1)

            def gates_of_kept(b):
                dve.wait_ge(s_tanh, b + 1)
                wait(dve, s_gT, b - 1)
                dve.scalar_tensor_tensor(gates[:, b % 2], margin[:, b % 2], 1.0, half_kept[:, b % 2],
                                         op0=ALU.add, op1=ALU.mult).then_inc(s_gate, 1)

            mid = {"C": residual, "F": first_norm, "Z": experts_norm, "G": z_lo, "J": choose_experts, "L": gates_of_kept}

            def w1_hi(e, p, banks_w=w_bank):
                dve.wait_ge(s_wT, e + 1)
                dve.tensor_scalar(w1_s[p][0][:], banks_w[0], scale_of(e), None, ALU.mult).then_inc(s_w1h, 1)

            def w1_lo(e, p, banks_w=w_bank):
                dve.wait_ge(s_w1h, e + 1)
                dve.scalar_tensor_tensor(w1_s[p][1][:], banks_w[0], scale_of(e), w1_s[p][0][:].bitcast(f32),
                                         op0=ALU.mult, op1=ALU.subtract).then_inc(s_w1s, 1)

            def w2_lo(e, p, banks_w=w_bank):
                dve.wait_ge(s_w2hi, e + 1)
                dve.tensor_tensor(w2_s[p][1][:], banks_w[1].rearrange("p (c n) -> p c n", c=HC), w2_s[p][0][:].bitcast(f32),
                                  ALU.subtract).then_inc(s_w2s, 1)

            def hidden_bias(e, p):
                dve.wait_ge(s_lb, e + 1)
                wait(dve, s_b1, e)
                dve.tensor_reduce(w1_lb_sum[:], w1_lb[:], AX.X, ALU.add).then_inc(s_lbs, 1)
                dve.wait_ge(s_lbs, e + 1)
                b1c = cols[:, C_B1:C_B1 + E * HC].rearrange("p (e c) -> p e c", e=E)[:, e, :]
                dve.tensor_tensor(b1_s[p][:], w1_lb_sum[:], b1c, ALU.add).then_inc(s_b1, 1)

            def scale_of(e):
                return cols[:, C_LS + e:C_LS + e + 1] if isinstance(e, int) else cols[:, C_LS:C_LS + E][:, bass.ds(e, 1)]

            def after(k):
                if k == -2:
                    w1_hi(0, 0, setup_w_bank)
                    w1_lo(0, 0, setup_w_bank)
                    w2_lo(0, 0, setup_w_bank)
                if k == 0:
                    dve.wait_ge(s_v1, 2)
                    v4 = v32[:].rearrange("p t (h e) -> p h t e", h=H)
                    dve.tensor_tensor(v_all[:, :, :, 2 * DH:3 * DH], v4, v_all[:, :, :, DH:2 * DH], ALU.subtract).then_inc(s_v_all, 1)
                    hidden_bias(0, 0)
                for name in AFTER_DVE.get(k, []):
                    mid[name[0]](int(name[1]))

            attention_steps(dve, step, after)

            def unit_step(unit):
                if isinstance(unit.rounds, int) and unit.rounds == 0:
                    for name in UNIT_DVE.get(unit.r, []):
                        mid[name[0]](int(name[1]))
                v = unit.ahead(W2_LAG)
                if v.real:
                    dve.wait_ge(s_hhi, v.u + 1)
                    dve.tensor_tensor(h_lo[:, v.r % NH, :], h32[:, v.r % NH, :], h_hi[:, v.r % NH, :].bitcast(f32),
                                      ALU.subtract).then_inc(s_hlo, 1)
                if unit.r < 0:
                    return
                if has_next(unit):
                    nxt = unit.ahead(UNITS)
                    for at, job in ((PREP_W1HI, w1_hi), (PREP_W1LO, w1_lo), (PREP_W2LO, w2_lo), (PREP_B1, hidden_bias)):
                        if unit.r % UNITS == at:
                            job(nxt.expert, nxt.parity)
                if unit.chunk == HC - 1:
                    n = unit.expert * B + unit.tile
                    tokens = slice(unit.tile * N, (unit.tile + 1) * N)
                    dve.wait_ge(s_used, (n + 1) * HC)
                    if is_first(unit):
                        dve.tensor_scalar(acc[:, tokens], y_bank[unit.tile % 2], cols[:, C_B2:C_B2 + 1], None, ALU.add).then_inc(s_yg, 1)
                        return
                    if unit.tile == 0:
                        dve.wait_ge(s_gb[unit.parity], 16 * unit.half + 16 * unit.parity)
                    wait(dve, s_acc, n - 1)
                    b2c = cols[:, C_B2:C_B2 + E]
                    b2c = b2c[:, unit.expert:unit.expert + 1] if isinstance(unit.expert, int) else b2c[:, bass.ds(unit.expert, 1)]
                    dve.scalar_tensor_tensor(y_g[:, unit.tile % 2, :], y_bank[unit.tile % 2], b2c, gate_b[unit.parity][:, tokens],
                                             op0=ALU.add, op1=ALU.mult).then_inc(s_yg, 1)

            expert_units(dve, unit_step)
            for b in range(B):
                q = b % 2
                dve.wait_ge(s_fT, b + 1)
                tiles = xs[:, b * JT:(b + 1) * JT, :]
                link(dve.tensor_tensor(x_pre[:, b], tiles_of(hid_bank[q]), tiles, ALU.add))
                moments(b, x_pre[:, b]).then_inc(s_fmv, 1)
                dve.wait_ge(s_frstd, b + 1)
                if b >= 2:
                    dve.wait_ge(s_out[b - 2], 16)
                normalise(x_out[:, q], b, x_pre[:, b]).then_inc(s_fin, 1)

        @block.tensor
        def _(pe):
            def three(dst, lhs, rhs, start=True, stop=True):
                pe.matmul(dst, lhs[0], rhs[0], start=start, stop=False)
                pe.matmul(dst, lhs[0], rhs[1], start=False, stop=False)
                return pe.matmul(dst, lhs[1], rhs[0], start=False, stop=stop)

            pe.wait_ge(s_const, 1)
            for n in range(JOBS):
                if n >= 8:
                    pe.wait_ge(s_sact, act_done(n - 8))
                    pe.wait_ge(s_sdve, dve_done(n - 8))
                bk = banks[n % 8]
                if n == 0:
                    pe.wait_ge(s_rows_in, 16 * 9)
                    ins = pe.transpose(bk[:, 0:C_ALL], rows[:], ident[0:C_ALL, 0:C_ALL])
                elif n < J_W:
                    b = n - J_X
                    pe.wait_ge(s_x_in[b], 16)
                    for j in range(JT):
                        ins = pe.transpose(bk[:, j * P:(j + 1) * P], xs[:, b * JT + j, :], ident[:])
                elif n < J_M:
                    i = n - J_W
                    pe.wait_ge(s_w_in[i // 2], 16)
                    for a in range(4):
                        ins = pe.transpose(bk[:, a * D:(a + 1) * D], w_raw[:, 4 * (i // 2) + a, (i % 2) * D:(i % 2 + 1) * D], ident[:])
                elif n < J_B:
                    i = n - J_M
                    pe.wait_ge(s_sact, act_done(J_W + 2 * (i // 2)))
                    pe.wait_ge(s_sdve, dve_done(J_W + 2 * (i // 2) + 1))
                    for a in range(2):
                        ins = pe.matmul(bk[:, a * 256:a * 256 + D + 1], wqT[:, 2 * i + a, :], wkT[:, 2 * i + a, :], start=True, stop=True)
                elif n == J_B:
                    for h in range(H):
                        pe.matmul(bk[:, h:h + 1], wkT[:, h, 0:D], cols[:, C_BQ + h:C_BQ + h + 1], start=True, stop=True)
                    pe.wait_ge(s_misc_in, 16 * 4)
                    pe.wait_ge(s_rw, 1)
                    pe.matmul(bk[:, H:H + H * DH], ones[0:1, :], row1[:, 0:H * DH], start=True, stop=True)
                    pe.matmul(bk[:, H + H * DH:H + VC], ones[:], bias_prod[:], start=True, stop=True)
                    pe.matmul(bk[:, H + VC:H + VC + D], ones[0:1, :], row1[:, H * DH:H * DH + D], start=True, stop=True)
                    rbk = bk[:, H + VC + D:H + VC + D + E]
                    pe.matmul(rbk, ones[0:1, :], row1[:, H * DH + D:], start=True, stop=False)
                    ins = pe.matmul(rbk, rlb_b[:], rwf[:], start=False, stop=True)
                else:
                    i = n - J_V
                    if i == 0:
                        pe.wait_ge(s_vcw, 1)
                    for a in range(2):
                        t = 2 * i + a
                        ins = three(bk[:, a * 256:a * 256 + VC], [w[:, t * P:(t + 1) * P] for w in xt], [w[:] for w in vc])
                ins.then_inc(s_fill, 1)

            def transpose_weights(e, half, p, banks_w=w_bank):
                pe.wait_ge(s_w1_in[p], 16 * half + 16)
                pe.wait_ge(s_w2_in[p], 16 * half + 16)
                wait(pe, s_w1s, e)
                wait(pe, s_w2s, e)
                for c in range(HC):
                    pe.transpose(banks_w[0][:, c * P:(c + 1) * P], w1_raw[p][:, c, :], ident[:])
                for c in range(HC):
                    ins = pe.transpose(banks_w[1][:, c * P:(c + 1) * P], w2_raw[p][:, c * P:(c + 1) * P], ident[:])
                ins.then_inc(s_wT, 1)

            pe.wait_ge(s_sdve, dve_done(JOBS - 7))
            transpose_weights(0, 0, 0, setup_w_bank)
            pe.wait_ge(s_sdve, dve_done(JOBS - 5))

            def step(k):
                s = k.at(-1)
                if s.real:
                    pe.wait_ge(s_thi, s.g + 1)
                    wait(pe, s_max, s.g)
                    for j in range(JT):
                        bk, at = R_AT[j]
                        dst = ps_rows[:, bk, at:at + (j + 1) * P]
                        pe.matmul(dst, t_s[0][:, s.r % 4, j * P:(j + 1) * P], xt[0][:, s.b * N:s.b * N + (j + 1) * P], start=True, stop=False)
                        ins = pe.matmul(ps_rows[:, bk, at + j * P:at + (j + 1) * P], ident16[:], future[:], start=False, stop=True)
                    ins.then_inc(s_rowsc, 1)
                s = k.at(3)
                if s.real:
                    pe.wait_ge(s_lo, s.g + 1)
                    if s.b == 0:
                        pe.wait_ge(s_v[s.parity], 16 * s.half + 16)
                    wait(pe, s_o, s.g)
                    for j in range(JT):
                        for m in range(j + 1):
                            at = T_AT[m] + (j - m) * P
                            for part, src in enumerate((p_hi, p_lo)):
                                ins = pe.matmul(ps_o[:, j * VS:j * VS + VW], src[:, s.r % NP, at:at + P],
                                                v_cur[s.parity][:, s.b * JT + m, 0:VW], start=(m == 0 and part == 0), stop=(m == j and part == 1))
                    ins.then_inc(s_pv, 1)
                s = k.at(-2)
                if s.real:
                    if s.b == 0:
                        pe.wait_ge(s_m[s.parity], 16 * s.half + 16)
                    wait(pe, s_tlo, s.g)
                    three(ps_t[:], [m_cur[s.parity][:, i, :] for i in range(2)], [w[:, s.b * N:(s.b + 1) * N] for w in xt]).then_inc(s_t, 1)
                s = k
                if s.real:
                    pe.wait_ge(s_tlo, s.g + 1)
                    wait(pe, s_exp, s.g)
                    for m in (0, 1, 3, 2):
                        n = (JT - m) * P
                        q0 = m * P
                        three(sT[:, T_AT[m]:T_AT[m] + n], [w[:, s.b * N + q0:s.b * N + q0 + P] for w in xt],
                              [w[:, s.r % 4, q0:N] for w in t_s], stop=False)
                        if m == 0:
                            pe.wait_ge(s_diag, s.g + 1)
                        ins = pe.matmul(sT[:, T_AT[m]:T_AT[m] + n], onesr[:], diag[s.r % 2][:].rearrange("p j n -> p (j n)")[:, q0:N],
                                        start=False, stop=True)
                    ins.then_inc(s_sT, 1)

            def transpose_sa(b, bk):
                pe.wait_ge(s_sa, G - B + b + 1)
                for j in range(JT):
                    ins = pe.transpose(bk[:, j * P:(j + 1) * P], sa_all[:, b * JT + j, :], ident[:])
                ins.then_inc(s_saT_ps, 1)

            def project(b, bk):
                pe.wait_ge(s_wp_in, 16)
                pe.wait_ge(s_saT, b + 1)
                for j in range(JT):
                    ins = pe.matmul(bk[:, j * P:(j + 1) * P], saT[:, b % 2, j * P:(j + 1) * P], wp_s[:], start=True, stop=True)
                ins.then_inc(s_att, 1)

            def transpose_z(b, bk):
                pe.wait_ge(s_z, b + 1)
                for j in range(JT):
                    ins = pe.transpose(bk[:, j * P:(j + 1) * P], z[:, b % 2, j, :], ident[:])
                ins.then_inc(s_zT, 1)

            def router(b, bk):
                pe.wait_ge(s_zlo, b + 1)
                for j in range(JT):
                    t = b * JT + j
                    ins = three(bk[:, j * E:(j + 1) * E], [w[:, t * P:(t + 1) * P] for w in xt], [w[:] for w in rw_s])
                ins.then_inc(s_lg, 1)

            def transpose_gates(b, bk):
                pe.wait_ge(s_gate, b + 1)
                for j in range(JT):
                    ins = pe.transpose(bk[0:E, j * P:(j + 1) * P], gates[:, b % 2, j, :], ident[:])
                ins.then_inc(s_gT, 1)

            stage = {"A": transpose_sa, "C": project, "G": transpose_z, "J": router, "M": transpose_gates}

            def mid(name):
                n = mid_order.index(name)
                if n >= 2:
                    before = mid_order[n - 2]
                    pe.wait_ge(mid_reader[before[0]], int(before[1]) + 1)
                else:
                    pe.wait_ge(s_max, G)
                stage[name[0]](int(name[1]), bank_of(name))

            def after(k):
                if k == -2:
                    pe.wait_ge(s_sdve, dve_done(JOBS - 1))
                if k == -1:
                    pe.wait_ge(s_w1s, 1)
                    pe.wait_ge(s_w2s, 1)
                for name in AFTER_PE.get(k, []):
                    mid(name)

            attention_steps(pe, step, after)
            pe.wait_ge(s_o, G)

            def unit_step(unit):
                if isinstance(unit.rounds, int) and unit.rounds == 0:
                    for name in UNIT_PE.get(unit.r, []):
                        mid(name)
                v = unit.ahead(W2_LAG)
                if v.real:
                    if v.r % UNITS == 0:
                        pe.wait_ge(s_w1s, v.expert + 1)
                    wait(pe, s_g, v.u - PH + 1)
                    c, t0 = v.chunk, v.tile * N
                    three(hid_bank_of(v), [w[:, c * P:(c + 1) * P] for w in w1_s[v.parity]], [w[:, t0:t0 + N] for w in xt]).then_inc(s_h, 1)
                if unit.r < 0:
                    return
                if unit.r % UNITS == 0:
                    pe.wait_ge(s_w2s, unit.expert + 1)
                pe.wait_ge(s_hlo, unit.u + 1)
                n = unit.expert * B + unit.tile
                if unit.chunk == 0:
                    wait(pe, s_yg, n - 1)
                ins = three(y_bank[unit.tile % 2], [w[:, unit.chunk, :] for w in w2_s[unit.parity]],
                            [w[:, unit.r % NH, :] for w in (h_hi, h_lo)], start=(unit.chunk == 0), stop=(unit.chunk == HC - 1))
                ins.then_inc(s_used, 1)
                if unit.r % UNITS == PREP_PE and has_next(unit):
                    nxt = unit.ahead(UNITS)
                    transpose_weights(nxt.expert, nxt.half, nxt.parity)

            expert_units(pe, unit_step)
            for b in range(B):
                pe.wait_ge(s_acc, (E - 1) * B + b + 1)
                if b >= 2:
                    pe.wait_ge(s_fmv, b - 1)
                for j in range(JT):
                    t = b * JT + j
                    ins = pe.transpose(hid_bank[b % 2][:, j * P:(j + 1) * P], acc[:, t * P:(t + 1) * P], ident[:])
                ins.then_inc(s_fT, 1)


_INS = ["L0_attn_x", "L0_attn_Wkqv", "L0_attn_bkqv", "L0_attn_Wp", "L0_attn_bp", "L0_ffn_router_ln_scale",
        "L0_ffn_router_ln_bias", "L0_ffn_router_w", "L0_ffn_router_b", "L0_ffn_expert_ln_scale",
        "L0_ffn_expert_ln_bias", "L0_ffn_w1", "L0_ffn_b1", "L0_ffn_w2", "L0_ffn_b2"]


def kernel(**inputs):
    import numpy as _np
    import concourse.bacc as _bacc
    from concourse import mybir as _mybir
    from concourse.bass_utils import run_bass_kernel_spmd as _run

    nc = _bacc.Bacc("TRN2", target_bir_lowering=False, num_devices=1)
    arrays, args = {}, []
    for name in _INS:
        a = _np.ascontiguousarray(inputs[name])
        arrays[f"in_{name}"] = a
        args.append(nc.dram_tensor(f"in_{name}", a.shape, _mybir.dt.from_np(a.dtype), kind="ExternalInput").ap())
    args.append(nc.dram_tensor("out", (B, N, D), _mybir.dt.float32, kind="ExternalOutput").ap())
    post_ln_layer(nc, *args)
    r = _run(nc, [arrays], core_ids=[0])
    return r.results[0]["out"]
```

```python
from contextlib import ExitStack

import numpy as np

import concourse.bass as bass
from concourse import mybir

B, N, D = 4, 512, 128
H, DH = 16, 8
E, HID = 8, 512
P = 128
JT = N // P
NT = B * JT
T = B * N
HC = HID // P
G = H * B
BLK = JT * (JT + 1) // 2
SC = BLK * P
VW = 3 * DH + 1
VS = 32
NP = 4
VC = H * DH + H
EPS_LN, EPS_MOE = 1e-5, 1e-6
MASKED = -1e30
P_SCALE = float(np.log(64.0))
T_AT = {0: 0, 1: 4 * P, 3: 7 * P, 2: 8 * P}
R_AT = {3: (0, 0), 2: (1, 0), 0: (1, 3 * P), 1: (2, 0)}

C_BK, C_BQ, C_LS, C_B2 = 0, H, 2 * H, 2 * H + E
C_B1 = C_B2 + E
C_RLB = C_B1 + E * HC
C_RLS = C_RLB + 1
C_RW = C_RLS + 1
C_ALL = C_RW + E
R_BV, R_BP, R_RB = 0, H * DH, H * DH + D
R_ALL = R_RB + E


class Step:

    def __init__(self, rounds, r):
        self.rounds, self.r = rounds, r

    def at(self, lag):
        return Step(self.rounds, self.r - lag)

    @property
    def g(self):
        return self.rounds * 8 + self.r

    @property
    def real(self):
        return not isinstance(self.rounds, int) or 0 <= self.g < G

    @property
    def b(self):
        return self.r % B

    @property
    def head(self):
        return self.rounds * 2 + self.r // B

    @property
    def half(self):
        return self.rounds + self.r // (2 * B)

    @property
    def parity(self):
        return (self.r // B) % 2


FIRST_STEP, LOOP_STEP, LAST_STEP = -2, 6, G + 2


def attention_steps(eng, emit, after, first=FIRST_STEP):
    for k in range(first, LOOP_STEP):
        emit(Step(0, k))
        after(k)
    rounds = G // 8 - 1
    with eng.Fori(0, rounds) as i:
        for r in range(LOOP_STEP, LOOP_STEP + 8):
            emit(Step(i, r))
    for r in range(LOOP_STEP, LAST_STEP - 8 * rounds + 1):
        emit(Step(rounds, r))
        after(8 * rounds + r)


def wait(eng, sem, value):
    if isinstance(value, int) and value <= 0:
        return
    eng.wait_ge(sem, value)


def post_ln_layer(nc, x, xT_in, wkT_in, wqT_in, wv_in, wp_in, columns, rows, elb, w1, w1T_in, w2T_in, out):
    f32, f32r = mybir.dt.float32, mybir.dt.float32r
    bf16, f16 = mybir.dt.bfloat16, mybir.dt.float16
    ACT, ALU, AX = mybir.ActivationFunctionType, mybir.AluOpType, mybir.AxisListType

    gates_dram = nc.dram_tensor("gates_by_expert", [E, T], f32, kind="Internal").ap()

    ctx = ExitStack()
    early = ExitStack()
    with ctx:
        def sb(name, shape, dt, stack=ctx):
            return stack.enter_context(nc.sbuf_tensor(name, shape, dt))

        def sem(name):
            return ctx.enter_context(nc.semaphore(name))

        ident = sb("ident", [P, P], f32)
        ident16 = sb("ident16", [P, P], bf16)
        future = sb("future", [P, P], bf16)
        ones = sb("ones", [P, P], f32)
        onesr = sb("onesr", [P, P], f32r)
        p_bias = sb("p_bias", [P, 1], f32)
        act_scratch = sb("act_scratch", [P, 1], f32)
        neg_half = sb("neg_half", [P, JT], f32)
        order = sb("order", [P, E, E], bf16)
        xs = sb("xs", [P, NT, D], f32)
        xt = [sb("xt_hi", [P, T], f32r), sb("xt_lo", [P, T], f32r)]
        cols = sb("cols", [P, C_ALL], f32)
        rw_s = sb("rw_s", [P, E], f32)
        rbias = sb("rbias", [P, E], f32)
        rlb_b = sb("rlb_b", [P, P], f32)
        row_bias = sb("row_bias", [P, R_ALL], f32)
        c_bias = sb("c_bias", [P, H], f32)
        wp_s = sb("wp_s", [D, D], f32)
        lb_b = sb("lb_b", [P, E, D], f32)
        sa_all = sb("sa_all", [P, NT, D], f32)
        w1_rows = [sb(f"w1_rows{p}", [P, HC, D], f32) for p in range(2)]
        w1_raw = [sb(f"w1_raw{p}", [D, HID], f32) for p in range(2)]
        w2_raw = [sb(f"w2_raw{p}", [P, HC, D], f32) for p in range(2)]
        w1_s = [[sb(f"w1_{n}{p}", [D, HID], f32r) for n in ("hi", "lo")] for p in range(2)]
        w2_s = [[sb(f"w2_{n}{p}", [P, HC, D], f32r) for n in ("hi", "lo")] for p in range(2)]
        w1_lb = sb("w1_lb", [P, HC, D], f32)
        w1_lb_sum = sb("w1_lb_sum", [P, HC], f32)
        b1_s = [sb(f"b1_s{p}", [P, HC], f32) for p in range(2)]

        saT = sb("saT", [P, 2, N], f32)
        x_pre = sb("x_pre", [P, B, JT, D], f32)
        z = sb("z", [P, 2, JT, D], f32)
        bn6 = sb("bn6", [P, B, JT, 6], f32)
        mv = sb("mv", [P, B, JT, 2], f32)
        var_eps = sb("var_eps", [P, B, JT], f32)
        rstd = sb("rstd", [P, B, JT], f32)
        rstd_z = sb("rstd_z", [P, B, JT], f32)
        neg_mean = sb("neg_mean", [P, B, JT], f32)
        offset = sb("offset", [P, B, JT], f32)
        logits = sb("logits", [P, 2, JT, E], f32)
        kept_logits = sb("kept_logits", [P, JT, E], f32)
        half_sum = sb("half_sum", [P, JT], f32)
        half_kept = sb("half_kept", [P, 2, JT, E], f32)
        margin = sb("margin", [P, 2, JT, E], f32)
        pair_gt = sb("pair_gt", [P, 2, JT, E, E], bf16)
        pair_eq = sb("pair_eq", [P, 2, JT, E, E], bf16)
        rank = sb("rank", [P, JT, E], f32)
        gates = sb("gates", [P, 2, JT, E], f32)
        gatesT = sb("gatesT", [E, T], f32)
        m_all = sb("m_all", [P, H, 2, D], f32r, early)
        v_all = sb("v_all", [P, H, NT, VS], bf16, early)
        s_all = sb("s_all", [P, H, 1 + NT], f32, early)
        m_cur = [sb(f"m_cur{p}", [P, 2, D], f32r, early) for p in range(2)]
        v_cur = [sb(f"v_cur{p}", [P, NT, VS], bf16, early) for p in range(2)]
        s_cur = [sb(f"s_cur{p}", [P, 1 + NT], f32, early) for p in range(2)]
        row_max = sb("row_max", [P, 4, JT], f32, early)
        row_tot = sb("row_tot", [P, 2, JT], f32, early)
        shift = sb("shift", [P, 2, JT], f32, early)
        diag = [sb(f"diag{p}", [P, JT + 1, P], f32r, early) for p in range(2)]
        o_rec = sb("o_rec", [P, 4, JT, VW], f32, early)
        o_inv = sb("o_inv", [P, 4, JT], f32, early)
        o_sum = sb("o_sum", [P, 2, JT, DH], f32, early)
        setup = ExitStack()
        wkT = sb("wkT", [D, H, D + 1], f32, setup)
        bias_prod = sb("bias_prod", [P, H], f32, setup)
        vc32 = sb("vc32", [P, VC], f32, setup)
        sb("gap", [P, 2 * SC - H * (D + 1) - H - VC], f32, setup)
        v32 = sb("v32", [P, NT, H * DH], f32, setup)
        wqT = sb("wqT", [D, H, D], f32, setup)
        x_T = sb("x_T", [P, T], f32, setup)
        setup.close()
        p32 = sb("p32", [P, NP, SC], f32, early)
        p_hi = sb("p_hi", [P, NP, SC], f16, early)
        p_lo = sb("p_lo", [P, NP, SC], f16, early)
        t_s = [sb("t_hi", [P, 4, N], f32r, early), sb("t_lo", [P, 4, N], f32r, early)]
        early.close()

        gate_b = [sb(f"gate_b{p}", [P, T], f32) for p in range(2)]
        NH = 4
        h32 = sb("h32", [P, NH, N], f32)
        h_hi = sb("h_hi", [P, NH, N], f32r)
        h_lo = sb("h_lo", [P, NH, N], f32r)
        y_g = sb("y_g", [P, 2, N], f32)
        acc = sb("acc", [P, T], f32)
        x_out = sb("x_out", [P, B, JT, D], f32)

        bank = [ctx.enter_context(nc.psum_tensor(f"bank{i}", [P, 512], f32)) for i in range(2)]
        ps_rows = ctx.enter_context(nc.psum_tensor("ps_rows", [P, 3, 512], f32))
        ps_sT = ctx.enter_context(nc.psum_tensor("ps_sT", [P, 3, 512], f32))
        ps_t, ps_o = bank
        banks = [ps_t[:, :], ps_o[:, :]] + [ps_rows[:, i, :] for i in range(3)] + [ps_sT[:, i, :] for i in range(3)]
        sT = ps_sT[:].rearrange("p a n -> p (a n)")[:, 0:SC]

        s_const = sem("const_ready")
        s_cols_in = sem("columns_loaded")
        s_rows_in = sem("rows_loaded")
        s_x_in = sem("x_loaded")
        s_xT_in = [sem(f"xT{b}_loaded") for b in range(B)]
        s_xhi, s_xlo = sem("xT_hi_ready"), sem("xT_lo_ready")
        s_w_in = [sem(f"w{i}_loaded") for i in range(2)]
        s_wv_in = sem("wv_loaded")
        s_lb_in = sem("expert_biases_loaded")
        s_wp_in = sem("wp_loaded")
        s_fill = sem("setup_bank_filled")
        s_sact = sem("setup_bank_read_by_scalar")
        s_sdve = sem("setup_bank_read_by_vector")
        s_vchain = sem("vector_chain")
        s_pchain = sem("pool_chain")
        s_v_all = sem("values_split")
        s_v1 = sem("v1_ready")
        s_v2 = sem("v2_ready")
        s_v_rest = sem("v_rest_ready")
        s_xbp = sem("x_plus_bp_ready")
        s_vcw = sem("vc_weights_ready")
        s_v32 = sem("v32_ready")
        s_rw = sem("router_weights_ready")
        s_m = [sem(f"m_of_head_here{p}") for p in range(2)]
        s_s = [sem(f"constants_of_head_here{p}") for p in range(2)]
        s_v = [sem(f"v_of_head_here{p}") for p in range(2)]
        s_t, s_thi, s_tlo = sem("t_ready"), sem("t_hi_ready"), sem("t_lo_ready")
        s_rowsc, s_max, s_diag = sem("row_scores_ready"), sem("row_max_ready"), sem("diag_ready")
        s_shift = sem("shift_steps")
        s_sT, s_exp, s_mask = sem("scoresT_ready"), sem("exp_ready"), sem("mask_ready")
        s_seen = sem("exp_seen_by_pool")
        s_hi, s_lo, s_pv, s_o = sem("p_hi_ready"), sem("p_lo_ready"), sem("pv_ready"), sem("o_saved")

        block = ctx.enter_context(nc.Block())

        J_B, J_V = H // 2, H // 2 + 1
        JOBS = J_V + NT // 2
        V_BANKS = (1, 5, 6, 7)
        X_SPLIT = (5, 6, 7, 8)
        EARLY_PE, EARLY_DVE = {0: -2, 3: -1}, {1: -2, 4: -1}

        def first_head(s):
            return isinstance(s.rounds, int) and s.head == 0

        def record(s):
            return 16 * s.half + 16 * s.parity

        def act_done(n):
            return min(n + 1, J_V)

        def dve_done(n):
            return n + 1

        s_inv, s_osum, s_sa = sem("o_inverse_ready"), sem("o_sum_steps"), sem("sa_ready")
        s_saT_ps, s_saT = sem("saT_in_bank"), sem("saT_ready")
        s_att, s_xpre = sem("attention_out_in_bank"), sem("x_pre_ready")
        s_mv = [sem(f"moments{b}_ready") for b in range(B)]
        s_rstd_z = [sem(f"rstd_of_both_norms{b}_ready") for b in range(B)]
        s_x1 = sem("first_norm_ready")
        s_z, s_zT, s_zhi, s_zlo = sem("z_ready"), sem("zT_in_bank"), sem("z_hi_ready"), sem("z_lo_ready")
        s_lg, s_lgs = sem("logits_in_bank"), sem("logits_ready")
        s_pairs = sem("logits_compared")
        s_margin, s_tanh = sem("margins_ready"), sem("tanh_ready")
        s_gate, s_gT, s_gTs = sem("gates_ready"), sem("gatesT_in_bank"), sem("gatesT_ready")
        s_gdram = [sem(f"gates{b}_in_dram") for b in range(B)]
        s_w1r_in = [sem(f"w1_rows_loaded{p}") for p in range(2)]
        s_w1_in = [sem(f"w1_loaded{p}") for p in range(2)]
        s_w2_in = [sem(f"w2_loaded{p}") for p in range(2)]
        s_gb0 = [sem(f"first_gates_broadcast{b}") for b in range(B)]
        s_gb1 = [sem(f"second_gates_broadcast{b}") for b in range(B)]
        s_gb = [sem(f"gates_broadcast{p}") for p in range(2)]
        s_w1s, s_w2hi, s_w2s = sem("w1_split"), sem("w2_hi_ready"), sem("w2_split")
        s_w1h = sem("w1_hi_ready")
        s_lb, s_lbs, s_b1 = sem("w1_lb_ready"), sem("w1_lb_summed"), sem("b1_ready")
        s_h, s_g, s_hhi, s_hlo = sem("hidden_in_bank"), sem("gelu_ready"), sem("h_hi_ready"), sem("h_lo_ready")
        s_used, s_yg, s_acc = sem("hidden_units_used"), sem("y_gated"), sem("acc_ready")
        s_offset = sem("offsets_ready")
        s_fT, s_fmv, s_frstd = sem("moe_out_in_bank"), sem("final_moments"), sem("final_rstd")
        s_fin = [sem(f"final{b}_ready") for b in range(B)]
        s_out = [sem(f"out{b}_stored") for b in range(B)]

        UNITS = B * HC
        PH = 4
        hid_bank = banks[0:2] + banks[4:6]
        mid_bank = banks[2:4]
        y_bank = banks[6:8]

        AFTER_PE = {63: ["A0"], 64: ["C0"], 65: ["A1", "C1"], 66: ["G0", "A2", "C2", "A3"]}
        AFTER_ACT = {63: ["A0"], 65: ["A1"], 66: ["G0", "A2", "A3"]}
        WITHIN_DVE = {64: ["C0"]}
        AFTER_DVE = {65: ["Z0"], 66: ["C1", "G0", "B0", "Z1", "C2"]}
        AFTER_POOL = {64: ["R0"], 65: ["B0"], 66: ["R1", "R2"]}
        UNIT_PE = {-3: ["C3"], -2: ["G1"], -1: ["J0"], 1: ["J1"], 3: ["G2"], 4: ["J2"], 6: ["G3"],
                   8: ["J3", "M0"], 11: ["M1"], 14: ["M2"], 17: ["M3"]}
        UNIT_ACT = {-2: ["G1"], 3: ["G2"], 5: ["L0"], 6: ["G3"], 8: ["L1", "M0"], 11: ["M1", "L2"],
                    14: ["M2", "L3"], 17: ["M3"]}
        UNIT_DVE = {-3: ["C3"], -2: ["G1", "Z2"], -1: ["J0"], 0: ["Z3"], 1: ["J1"], 3: ["G2"],
                    4: ["J2"], 6: ["G3", "L0"], 8: ["J3"], 9: ["L1"], 12: ["L2"], 15: ["L3"]}
        UNIT_POOL = {-3: ["R3"], 0: ["K0"], 4: ["K1"], 5: ["K2"], 8: ["K3"], 11: ["Y0"],
                     14: ["Y1"], 15: ["Y2"], 17: ["Y3"], 20: ["F0"], 24: ["F1"]}
        LAST_PE, END_PE = {23: ["T0"], 27: ["T1"]}, ["T2", "T3"]
        LAST_DVE, END_DVE = {24: ["U0"], 29: ["U1"]}, ["U2", "U3", "V3"]
        END_ACT = ["V0", "V1", "V2"]
        LAST_POOL, END_POOL = {2: ["F2"], 10: ["F3"], 25: ["W0"], 29: ["W1"]}, ["W2", "W3"]
        mid_order = [x for t in (AFTER_PE, UNIT_PE) for k in sorted(t) for x in t[k] if x[0] != "C"]
        mid_reader = {"A": s_saT, "G": s_zlo, "J": s_lgs, "M": s_gTs}

        class Unit:

            def __init__(self, rounds, r):
                self.rounds, self.r = rounds, r

            def ahead(self, n):
                return Unit(self.rounds, self.r + n)

            @property
            def u(self):
                return self.rounds * (2 * UNITS) + self.r

            @property
            def real(self):
                return not isinstance(self.rounds, int) or 0 <= self.u < E * UNITS

            @property
            def expert(self):
                return self.rounds * 2 + self.r // UNITS

            @property
            def parity(self):
                return (self.r // UNITS) % 2

            @property
            def half(self):
                return self.rounds + self.r // (2 * UNITS)

            @property
            def tile(self):
                return (self.r // HC) % B

            @property
            def chunk(self):
                return self.r % HC

        def hid_bank_of(unit):
            return hid_bank[unit.r % PH]

        W2_LAG = 3
        PREP_W1HI, PREP_W1LO, PREP_W2HI, PREP_W2LO, PREP_B1 = 4, 5, 5, 6, 8

        def expert_units(eng, emit):
            for r in range(-W2_LAG, 0):
                emit(Unit(0, r))
            for r in range(2 * UNITS):
                emit(Unit(0, r))
            rounds = E // 2 - 1
            with eng.Fori(1, rounds) as i:
                for r in range(2 * UNITS):
                    emit(Unit(i, r))
            for r in range(2 * UNITS):
                emit(Unit(rounds, r))

        def work_between(unit, first, last, mid):
            if isinstance(unit.rounds, int):
                for name in (first if unit.rounds == 0 else last).get(unit.r, []):
                    mid(name)

        def has_next(unit, n=1):
            return not isinstance(unit.rounds, int) or unit.expert + n < E

        def is_end(unit):
            return isinstance(unit.rounds, int) and unit.u == E * UNITS - 1

        def is_first(unit):
            return isinstance(unit.rounds, int) and unit.expert == 0

        def bank_of(name):
            if name[0] == "C":
                return banks[4 + int(name[1])]
            return mid_bank[mid_order.index(name) % 2]

        def tiles_of(bk):
            return bk.rearrange("p (j n) -> p j n", j=JT)

        @block.sync
        def _(sp):
            sp.dma_start(cols[:], columns).then_inc(s_cols_in, 16)
            for i in range(2):
                sp.dma_start(wkT[:, 8 * i:8 * i + 8, :], wkT_in[:, 8 * i:8 * i + 8, :]).then_inc(s_w_in[i], 16)
            for b in range(B):
                sp.dma_start(x_T[:, b * N:(b + 1) * N], xT_in[:, b * N:(b + 1) * N]).then_inc(s_xT_in[b], 16)
            sp.dma_start(vc32[:, 0:H * DH], wv_in).then_inc(s_wv_in, 16)
            sp.dma_start(row_bias[:], rows.unsqueeze(0).to_broadcast([P, R_ALL])).then_inc(s_rows_in, 16)
            sp.dma_start(xs[:], x.rearrange("b (j p) d -> p (b j) d", p=P)).then_inc(s_x_in, 16)
            sp.dma_start(wp_s[:], wp_in).then_inc(s_wp_in, 16)
            sp.dma_start(lb_b[:], elb.unsqueeze(0).to_broadcast([P, E, D])).then_inc(s_lb_in, 16)

            def load_weights(e, p):
                sp.dma_start(w1_raw[p][:], w1T_in[e]).then_inc(s_w1_in[p], 16)
                sp.dma_start(w2_raw[p][:], w2T_in[e].rearrange("(c h) d -> h c d", c=HC)).then_inc(s_w2_in[p], 16)
                sp.dma_start(w1_rows[p][:], w1[e].rearrange("(c h) d -> h c d", c=HC)).then_inc(s_w1r_in[p], 16)

            def raw_weights_used(n):
                sp.wait_ge(s_w1s, n)
                sp.wait_ge(s_w2s, n)
                sp.wait_ge(s_lb, n)

            load_weights(0, 0)
            load_weights(1, 1)

            def head(rounds, hh):
                h = rounds * 2 + hh
                p = hh % 2
                first = isinstance(rounds, int)
                if first:
                    sp.wait_ge(s_sact, act_done(J_B))
                    sp.wait_ge(s_sdve, dve_done(J_B - 1))
                else:
                    sp.wait_ge(s_t, h * 4 - 4)
                sp.dma_start(m_cur[p][:].bitcast(f32), m_all[:, h, :, :].bitcast(f32)).then_inc(s_m[p], 16)
                if first:
                    sp.wait_ge(s_sdve, dve_done(JOBS - 1))
                else:
                    sp.wait_ge(s_tlo, h * 4 - 4)
                    sp.wait_ge(s_diag, h * 4 - 4)
                sp.dma_start(s_cur[p][:], s_all[:, h, :]).then_inc(s_s[p], 16)

            def head_values(rounds, hh):
                h = rounds * 2 + hh
                p = hh % 2
                if isinstance(rounds, int):
                    sp.wait_ge(s_v_all, 1)
                else:
                    sp.wait_ge(s_pv, h * 4 - 4)
                sp.dma_start(v_cur[p][:], v_all[:, h, :, :]).then_inc(s_v[p], 16)

            head(0, 1)
            for hh in range(2):
                head_values(0, hh)
            sp.wait_ge(s_v_all, 2)
            with sp.Fori(1, H // 2) as i:
                for hh in range(2):
                    head(i, hh)
                    head_values(i, hh)

            def load_gates(e, p):
                sp.dma_start(gate_b[p][:], gates_dram[e, :].unsqueeze(0).to_broadcast([P, T])).then_inc(s_gb[p], 16)

            raw_weights_used(1)
            load_weights(2, 0)
            sp.wait_ge(s_o, G)
            for b in range(B):
                t0 = b * N
                sp.wait_ge(s_gTs, b + 1)
                sp.dma_start(gates_dram[:, t0:t0 + N], gatesT[:, t0:t0 + N]).then_inc(s_gdram[b], 16)
                sp.wait_ge(s_gdram[b], 16)
                for e, s_gb_e in enumerate((s_gb0, s_gb1)):
                    sp.dma_start(gate_b[e][:, t0:t0 + N], gates_dram[e, t0:t0 + N].unsqueeze(0).to_broadcast([P, N])).then_inc(s_gb_e[b], 16)

            def next_loads(unit):
                if unit.r % UNITS == 0 and has_next(unit) and not is_first(unit):
                    e = unit.expert + 1
                    wait(sp, s_acc, (e - 1) * B)
                    load_gates(e, 1 - unit.parity)
                if unit.r % UNITS == 2 * HC and has_next(unit, 2) and not is_first(unit):
                    raw_weights_used(unit.expert + 1)
                    load_weights(unit.expert + 2, unit.parity)

            expert_units(sp, lambda unit: next_loads(unit) if unit.r >= 0 else None)
            for b in range(B):
                sp.wait_ge(s_fin[b], 1)
                sp.dma_start(out[b].rearrange("(j p) d -> p j d", p=P), x_out[:, b, :, :]).then_inc(s_out[b], 16)
            for b in range(B):
                sp.wait_ge(s_out[b], 16)

        @block.gpsimd
        def _(pool):
            done = [0]

            def link(ins):
                done[0] += 1
                ins.then_inc(s_pchain, 1)
                pool.wait_ge(s_pchain, done[0])

            pool.memset(ones[:], 1.0)
            pool.memset(p_bias[:], P_SCALE)
            pool.memset(neg_half[:], -0.5)
            pool.memset(order[:], 1.0)
            pool.memset(future[:], 0.0)
            pool.memset(ident16[:], 0.0)
            link(pool.memset(ident[:], 0.0))
            pool.affine_select(out=ident[:], in_=ident[:], compare_op=ALU.not_equal, fill=1.0, base=0,
                               pattern=[[-1, P]], channel_multiplier=1)
            pool.affine_select(out=ident16[:], in_=ident16[:], compare_op=ALU.not_equal, fill=1.0, base=0,
                               pattern=[[-1, P]], channel_multiplier=1)
            pool.affine_select(out=future[:], in_=future[:], compare_op=ALU.is_ge, fill=MASKED, base=0,
                               pattern=[[-1, P]], channel_multiplier=1)
            pool.affine_select(out=order[:], in_=order[:], compare_op=ALU.is_ge, fill=0.0, base=-1,
                               pattern=[[1, E], [-1, E]], channel_multiplier=0).then_inc(s_const, 1)

            ident_b = ident[:].unsqueeze(1).to_broadcast([P, JT, P])

            v4 = v32[:].rearrange("p t (h e) -> p h t e", h=H)

            def subtract_v1(b):
                pool.wait_ge(s_v1, b + 1)
                ts = slice(b * JT, (b + 1) * JT)
                pool.tensor_tensor(v4[:, :, ts], v4[:, :, ts], v_all[:, :, ts, 0:DH], ALU.subtract).then_inc(s_v_rest, 1)

            def bias_product(e, half, p):
                pool.wait_ge(s_w1r_in[p], 16 * half + 16)
                wait(pool, s_lbs, e)
                pool.tensor_tensor(w1_lb[:], w1_rows[p][:], lb_b[:, e, :].unsqueeze(1).to_broadcast([P, HC, D]),
                                   ALU.mult).then_inc(s_lb, 1)

            def step(k):
                s = k.at(1)
                if s.real:
                    pool.wait_ge(s_exp, s.g + 1)
                    pool.sem_inc(s_seen, 1)
                    for at in (0, 7 * P):
                        stride = 4 * P if at == 0 else P
                        view = p32[:, s.r % NP, at:at + 2 * stride].rearrange("p (a n) -> p a n", a=2)[:, :, 0:P]
                        ins = pool.affine_select(out=view, in_=view, compare_op=ALU.is_ge, fill=0.0, base=0,
                                                 pattern=[[0, 2], [1, P]], channel_multiplier=-1)
                    ins.then_inc(s_mask, 1)
                s = k.at(-1)
                if s.real:
                    q = s.r % 2
                    if first_head(s):
                        pool.wait_ge(s_sdve, dve_done(J_V + 2 * s.b + 1))
                    elif s.b == 0:
                        pool.wait_ge(s_s[s.parity], record(s))
                    pool.wait_ge(s_max, s.g + 1)
                    wait(pool, s_shift, 2 * s.g - 2)
                    c = (s_all[:, 0] if first_head(s) else s_cur[s.parity])[:, 1 + s.b * JT:1 + (s.b + 1) * JT]
                    pool.tensor_tensor(row_tot[:, q, :], row_max[:, s.r % 4, :], c, ALU.add).then_inc(s_shift, 1)
                    pool.wait_ge(s_shift, 2 * s.g + 1)
                    pool.tensor_tensor(shift[:, q, :], c, row_tot[:, q, :], ALU.subtract).then_inc(s_shift, 1)
                    pool.wait_ge(s_shift, 2 * s.g + 2)
                    wait(pool, s_sT, s.g - 1)
                    pool.tensor_tensor(diag[q][:, 0:JT, :], ident_b, shift[:, q, :].unsqueeze(2).to_broadcast([P, JT, P]), ALU.mult)
                    pool.tensor_tensor(diag[q][:, JT, :], ident[:], shift[:, q, JT - 1:JT].to_broadcast([P, P]), ALU.mult).then_inc(s_diag, 1)

            def heads_output(k):
                s = k.at(3)
                if s.real:
                    q = s.r % 4
                    pool.wait_ge(s_inv, s.g + 1)
                    pool.tensor_tensor(o_sum[:, q % 2], o_rec[:, q, :, 0:DH], o_rec[:, q, :, DH:2 * DH], ALU.add).then_inc(s_osum, 1)
                    pool.wait_ge(s_osum, 2 * s.g + 1)
                    pool.tensor_tensor(o_sum[:, q % 2], o_sum[:, q % 2], o_rec[:, q, :, 2 * DH:3 * DH], ALU.add).then_inc(s_osum, 1)
                    pool.wait_ge(s_osum, 2 * s.g + 2)
                    dst = sa_all[:, s.b * JT:(s.b + 1) * JT, :].rearrange("p j (h e) -> p j h e", h=H)[:, :, s.head, :]
                    pool.tensor_tensor(dst, o_sum[:, q % 2], o_inv[:, q].unsqueeze(2).to_broadcast([P, JT, DH]), ALU.mult).then_inc(s_sa, 1)

            def inv_std(b, dst, scale, eps):
                link(pool.tensor_scalar(var_eps[:, b, :], mv[:, b, :, 1], scale, eps, ALU.mult, ALU.add))
                return pool.tensor_tensor(dst[:, b, :], var_eps[:, b, :], neg_half[:], ALU.pow)

            def both_inv_std(b):
                pool.wait_ge(s_mv[b], 1)
                inv_std(b, rstd_z, 1.0 + EPS_MOE, EPS_LN * EPS_MOE).then_inc(s_rstd_z[b], 1)

            def first_norm(b):
                link(inv_std(b, rstd, 1.0, EPS_LN))
                for j in range(JT):
                    ins = pool.tensor_scalar(xs[:, b * JT + j, :], x_pre[:, b, j, :], mv[:, b, j, 0:1], rstd[:, b, j:j + 1],
                                             ALU.subtract, ALU.mult)
                ins.then_inc(s_x1, 1)

            def last_inv_std(b):
                pool.wait_ge(s_fmv, b + 1)
                inv_std(b, rstd, 1.0, EPS_LN).then_inc(s_frstd, 1)
                if f"V{b}" in END_ACT:
                    pool.wait_ge(s_frstd, b + 1)
                    link(pool.tensor_scalar(neg_mean[:, b, :], mv[:, b, :, 0], -1.0, None, ALU.mult))
                    pool.tensor_tensor(offset[:, b, :], neg_mean[:, b, :], rstd[:, b, :], ALU.mult).then_inc(s_offset, 1)

            def choose_experts(b):
                pool.wait_ge(s_pairs, b + 1)
                wait(pool, s_gate, b - 1)
                lg, half = logits[:, b % 2], half_kept[:, b % 2]
                gt, eq = pair_gt[:, b % 2], pair_eq[:, b % 2]
                link(pool.tensor_tensor(eq.rearrange("p j a b -> p j (a b)"), eq.rearrange("p j a b -> p j (a b)"),
                                        order[:].rearrange("p a b -> p (a b)").unsqueeze(1).to_broadcast([P, JT, E * E]), ALU.mult))
                link(pool.tensor_tensor(gt, gt, eq, ALU.add))
                n = E // 2
                while n > 1:
                    link(pool.tensor_tensor(gt[:, :, :, 0:n], gt[:, :, :, 0:n], gt[:, :, :, n:2 * n], ALU.add))
                    n //= 2
                link(pool.tensor_tensor(rank[:], gt[:, :, :, 0], gt[:, :, :, 1], ALU.add))
                link(pool.tensor_scalar(half, rank[:], 1.5, 0.5, ALU.is_lt, ALU.mult))
                link(pool.tensor_tensor(kept_logits[:], half, lg, ALU.mult))
                n = E // 2
                while n > 1:
                    link(pool.tensor_tensor(kept_logits[:, :, 0:n], kept_logits[:, :, 0:n], kept_logits[:, :, n:2 * n], ALU.add))
                    n //= 2
                link(pool.tensor_tensor(half_sum[:], kept_logits[:, :, 0], kept_logits[:, :, 1], ALU.add))
                pool.tensor_tensor(margin[:, b % 2], lg, half_sum[:].unsqueeze(2).to_broadcast([P, JT, E]),
                                   ALU.subtract).then_inc(s_margin, 1)

            def gate_first_expert(b):
                pool.wait_ge(s_yg, b + 1)
                pool.wait_ge(s_gb0[b], 16)
                tokens = acc[:, b * N:(b + 1) * N]
                pool.tensor_tensor(tokens, tokens, gate_b[0][:, b * N:(b + 1) * N], ALU.mult).then_inc(s_acc, 1)

            def first_bias_product(_):
                pool.wait_ge(s_lb_in, 16)
                bias_product(0, 0, 0)

            mid = {"R": both_inv_std, "B": first_bias_product, "F": first_norm, "K": choose_experts, "Y": gate_first_expert, "W": last_inv_std}

            def do(name):
                mid[name[0]](int(name[1]))

            def full_step(k):
                step(k)
                heads_output(k)

            def after(k):
                if k == -1:
                    subtract_v1(2)
                    subtract_v1(3)
                for name in AFTER_POOL.get(k, []):
                    do(name)

            pool.wait_ge(s_x_in, 16)
            pool.wait_ge(s_rows_in, 16)
            for b in range(B):
                tiles = xs[:, b * JT:(b + 1) * JT, :]
                pool.tensor_tensor(tiles, tiles, row_bias[:, R_BP:R_BP + D].unsqueeze(1).to_broadcast([P, JT, D]),
                                   ALU.add).then_inc(s_xbp, 1)
            subtract_v1(0)
            subtract_v1(1)
            attention_steps(pool, full_step, after)

            def unit_step(unit):
                work_between(unit, UNIT_POOL, LAST_POOL, do)
                if unit.r < 0:
                    return
                if unit.r % UNITS == 2 and has_next(unit):
                    nxt = unit.ahead(UNITS)
                    bias_product(nxt.expert, nxt.half, nxt.parity)
                if unit.chunk == HC - 1 and not is_first(unit) and not is_end(unit):
                    n = unit.expert * B + unit.tile
                    tokens = slice(unit.tile * N, (unit.tile + 1) * N)
                    pool.wait_ge(s_yg, n + 1)
                    wait(pool, s_acc, n)
                    pool.tensor_tensor(acc[:, tokens], acc[:, tokens], y_g[:, unit.tile % 2, :], ALU.add).then_inc(s_acc, 1)

            expert_units(pool, unit_step)
            for name in END_POOL:
                do(name)

        @block.scalar
        def _(act):
            for i in range(2):
                act.dma_start(wqT[:, 8 * i:8 * i + 8, :], wqT_in[:, 8 * i:8 * i + 8, :]).then_inc(s_w_in[i], 16)
            act.wait_ge(s_const, 1)
            act.activation(act_scratch[:], p_bias[:], ACT.Exp)
            for n in range(J_V):
                act.wait_ge(s_fill, n + 1)
                bk = banks[n % 8]
                if n < J_B:
                    act.activation(m_all[:, 2 * n:2 * n + 2, 0, :], bk.rearrange("p (a n) -> p a n", a=2)[:, :, 0:D], ACT.Copy).then_inc(s_sact, 1)
                else:
                    act.activation(s_all[:, :, 0], bk[:, 0:H], ACT.Copy).then_inc(s_sact, 1)
                if n in X_SPLIT:
                    b = X_SPLIT.index(n)
                    act.wait_ge(s_xT_in[b], 16)
                    act.activation(xt[0][:, b * N:(b + 1) * N], x_T[:, b * N:(b + 1) * N], ACT.Copy).then_inc(s_xhi, 1)
            v4 = v32[:].rearrange("p t (h e) -> p h t e", h=H)

            def v1(b):
                act.wait_ge(s_v32, 2 * b + 2)
                ts = slice(b * JT, (b + 1) * JT)
                act.activation(v_all[:, :, ts, 0:DH], v4[:, :, ts], ACT.Copy).then_inc(s_v1, 1)

            def v2(b):
                act.wait_ge(s_v_rest, b + 1)
                ts = slice(b * JT, (b + 1) * JT)
                act.activation(v_all[:, :, ts, DH:2 * DH], v4[:, :, ts], ACT.Copy).then_inc(s_v2, 1)

            def step(k):
                s = k.at(1)
                if s.real:
                    act.wait_ge(s_sT, s.g + 1)
                    wait(act, s_lo, s.g - NP + 1)
                    act.activation(p32[:, s.r % NP, :], sT, ACT.Exp, bias=p_bias[:], scale=float(D) ** -0.5).then_inc(s_exp, 1)
                s = k.at(3)
                if s.real:
                    act.wait_ge(s_pv, s.g + 1)
                    wait(act, s_sa, s.g - 2)
                    act.activation(o_rec[:, s.r % 4], ps_o[:, 0:JT * VS].rearrange("p (j e) -> p j e", j=JT)[:, :, 0:VW],
                                   ACT.Copy).then_inc(s_o, 1)
                s = k.at(-2)
                if s.real:
                    if first_head(s):
                        act.wait_ge(s_sact, act_done(J_B))
                    elif s.b == 0:
                        act.wait_ge(s_s[s.parity], record(s))
                    act.wait_ge(s_t, s.g + 1)
                    wait(act, s_sT, s.g - 3)
                    act.activation(t_s[0][:, s.r % 4, :], ps_t[:], ACT.Identity,
                                   bias=(s_all[:, 0] if first_head(s) else s_cur[s.parity])[:, 0:1]).then_inc(s_thi, 1)
                s = k.at(1)
                if s.real:
                    act.wait_ge(s_mask, s.g + 1)
                    wait(act, s_pv, s.g - NP + 1)
                    act.activation(p_hi[:, s.r % NP, :], p32[:, s.r % NP, :], ACT.Copy).then_inc(s_hi, 1)

            def w2_hi(e, half, p):
                act.wait_ge(s_w2_in[p], 16 * half + 16)
                act.activation(w2_s[p][0][:], w2_raw[p][:], ACT.Copy).then_inc(s_w2hi, 1)

            def copy_saT(b):
                act.wait_ge(s_saT_ps, b + 1)
                wait(act, s_att, b - 1)
                act.activation(saT[:, b % 2, :], bank_of(f"A{b}"), ACT.Copy).then_inc(s_saT, 1)

            def z_hi(b):
                act.wait_ge(s_zT, b + 1)
                act.activation(xt[0][:, b * N:(b + 1) * N], bank_of(f"G{b}"), ACT.Copy).then_inc(s_zhi, 1)

            def tanh_of_margins(b):
                act.wait_ge(s_margin, b + 1)
                act.activation(margin[:, b % 2], margin[:, b % 2], ACT.Tanh).then_inc(s_tanh, 1)

            def copy_gatesT(b):
                act.wait_ge(s_gT, b + 1)
                act.activation(gatesT[:, b * N:(b + 1) * N], bank_of(f"M{b}")[0:E, :], ACT.Copy).then_inc(s_gTs, 1)

            def last_norm(b):
                act.wait_ge(s_offset, b + 1)
                for j in range(JT):
                    ins = act.activation(x_out[:, b, j, :], x_pre[:, b, j, :], ACT.Identity, bias=offset[:, b, j:j + 1], scale=rstd[:, b, j:j + 1])
                ins.then_inc(s_fin[b], 1)

            mid = {"V": last_norm, "A": copy_saT, "G": z_hi, "L": tanh_of_margins, "M": copy_gatesT}

            def do(name):
                mid[name[0]](int(name[1]))

            def after(k):
                if k == 62:
                    w2_hi(0, 0, 0)
                if k == 0:
                    v2(3)
                if k == 2:
                    act.wait_ge(s_v_all, 2)
                for name in AFTER_ACT.get(k, []):
                    do(name)
                    if name == "A1":
                        act.activation(act_scratch[:], p_bias[:], ACT.Gelu)

            step(Step(0, -2))
            v1(0)
            v1(1)
            step(Step(0, -1))
            for b in range(2):
                v2(b)
                v1(b + 2)
            v2(2)
            attention_steps(act, step, after, first=0)

            def unit_step(unit):
                work_between(unit, UNIT_ACT, {}, do)
                v = unit.ahead(W2_LAG)
                if v.real:
                    act.wait_ge(s_h, v.u + 1)
                    if v.r % UNITS == 0:
                        act.wait_ge(s_b1, v.expert + 1)
                    wait(act, s_used, v.u - NH + 1)
                    act.activation(h32[:, v.r % NH, :], hid_bank_of(v), ACT.Gelu,
                                   bias=b1_s[v.parity][:, v.chunk:v.chunk + 1]).then_inc(s_g, 1)
                    act.wait_ge(s_g, v.u + 1)
                    act.activation(h_hi[:, v.r % NH, :], h32[:, v.r % NH, :], ACT.Copy).then_inc(s_hhi, 1)
                if unit.r >= 0 and unit.r % UNITS == PREP_W2HI and has_next(unit):
                    nxt = unit.ahead(UNITS)
                    w2_hi(nxt.expert, nxt.half, nxt.parity)

            expert_units(act, unit_step)
            for name in END_ACT:
                do(name)

        @block.vector
        def _(dve):
            done = [0]

            def link(ins):
                done[0] += 1
                ins.then_inc(s_vchain, 1)
                dve.wait_ge(s_vchain, done[0])

            dve.wait_ge(s_const, 1)
            link(dve.tensor_copy(onesr[:], ones[:]))
            dve.memset(v_all[:, :, :, 3 * DH:VS], 1.0)
            def step(k):
                s = k.at(-1)
                if s.real:
                    dve.wait_ge(s_rowsc, s.g + 1)
                    wait(dve, s_diag, s.g - 3)
                    for j in range(JT):
                        bk, at = R_AT[j]
                        ins = dve.tensor_reduce(row_max[:, s.r % 4, j:j + 1], ps_rows[:, bk, at:at + (j + 1) * P], AX.X, ALU.max)
                    ins.then_inc(s_max, 1)
                s = k.at(-2)
                if s.real:
                    if first_head(s):
                        dve.wait_ge(s_sact, act_done(J_B))
                    elif s.b == 0:
                        dve.wait_ge(s_s[s.parity], record(s))
                    dve.wait_ge(s_thi, s.g + 1)
                    dve.scalar_tensor_tensor(t_s[1][:, s.r % 4, :], ps_t[:], (s_all[:, 0] if first_head(s) else s_cur[s.parity])[:, 0:1], t_s[0][:, s.r % 4, :].bitcast(f32),
                                             op0=ALU.add, op1=ALU.subtract).then_inc(s_tlo, 1)
                s = k.at(3)
                if s.real:
                    dve.wait_ge(s_o, s.g + 1)
                    dve.reciprocal(o_inv[:, s.r % 4], o_rec[:, s.r % 4, :, 3 * DH]).then_inc(s_inv, 1)
                for name in WITHIN_DVE.get(k.g, []) if isinstance(k.rounds, int) else []:
                    do(name)
                s = k.at(1)
                if s.real:
                    dve.wait_ge(s_hi, s.g + 1)
                    wait(dve, s_pv, s.g - NP + 1)
                    dve.tensor_tensor(p_lo[:, s.r % NP, :], p32[:, s.r % NP, :], p_hi[:, s.r % NP, :], ALU.subtract).then_inc(s_lo, 1)

            dve.wait_ge(s_cols_in, 16)
            dve.tensor_tensor(bias_prod[:], cols[:, C_BK:C_BK + H], cols[:, C_BQ:C_BQ + H], ALU.mult)
            dve.tensor_scalar(rw_s[:], cols[:, C_RW:C_RW + E], cols[:, C_RLS:C_RLS + 1], None, ALU.mult)
            dve.tensor_copy(rlb_b[:], cols[:, C_RLB:C_RLB + 1].to_broadcast([P, P])).then_inc(s_rw, 1)
            for n in range(JOBS):
                dve.wait_ge(s_fill, n + 1)
                bk = banks[n % 8 if n < J_V else V_BANKS[(n - J_V) % 4]]
                v = bk.rearrange("p (a n) -> p a n", a=2)
                if n < J_B:
                    dve.wait_ge(s_sact, act_done(n))
                    ins = dve.tensor_copy(vc32[:, H * DH + 2 * n:H * DH + 2 * n + 2], v[:, :, D])
                    if n == J_B - 1:
                        ins.then_inc(s_vcw, 1)
                    dve.tensor_tensor(m_all[:, 2 * n:2 * n + 2, 1, :], v[:, :, 0:D],
                                      m_all[:, 2 * n:2 * n + 2, 0, :].bitcast(f32), ALU.subtract).then_inc(s_sdve, 1)
                elif n == J_B:
                    dve.wait_ge(s_sact, act_done(n))
                    dve.wait_ge(s_rows_in, 16)
                    dve.tensor_tensor(rbias[:], bk[:, 2 * H:2 * H + E], row_bias[:, R_RB:R_RB + E], ALU.add)
                    dve.tensor_copy(c_bias[:], bk[:, H:2 * H]).then_inc(s_sdve, 1)
                    dve.wait_ge(s_sdve, dve_done(n))
                else:
                    i = n - J_V
                    dve.tensor_tensor(v32[:, 2 * i:2 * i + 2, :], v[:, :, 0:H * DH],
                                      row_bias[:, R_BV:R_BV + H * DH].unsqueeze(1).to_broadcast([P, 2, H * DH]), ALU.add).then_inc(s_v32, 1)
                    dve.tensor_tensor(s_all[:, :, 1 + 2 * i:3 + 2 * i].rearrange("p h a -> p a h"), v[:, :, H * DH:VC],
                                      c_bias[:].unsqueeze(1).to_broadcast([P, 2, H]), ALU.add).then_inc(s_sdve, 1)
                    if i in EARLY_DVE:
                        step(Step(0, EARLY_DVE[i]))
                if n in X_SPLIT:
                    b = X_SPLIT.index(n)
                    dve.wait_ge(s_xhi, b + 1)
                    dve.tensor_tensor(xt[1][:, b * N:(b + 1) * N], x_T[:, b * N:(b + 1) * N], xt[0][:, b * N:(b + 1) * N].bitcast(f32),
                                      ALU.subtract).then_inc(s_xlo, 1)

            def moments(n, tiles):
                for j in range(JT):
                    ins = dve.bn_stats(bn6[:, n, j, :], tiles[:, j, :])
                link(ins)
                for j in range(JT):
                    ins = dve.bn_aggr(mv[:, n, j, :], bn6[:, n, j, :])
                return ins

            def normalise(dst, n, tiles, inv_std):
                for j in range(JT):
                    ins = dve.tensor_scalar(dst[:, j, :], tiles[:, j, :], mv[:, n, j, 0:1], inv_std[:, n, j:j + 1],
                                            ALU.subtract, ALU.mult)
                return ins

            def residual(b):
                dve.wait_ge(s_att, b + 1)
                dve.wait_ge(s_xbp, b + 1)
                dve.tensor_tensor(x_pre[:, b], tiles_of(bank_of(f"C{b}")), xs[:, b * JT:(b + 1) * JT, :], ALU.add).then_inc(s_xpre, 1)
                dve.wait_ge(s_xpre, b + 1)
                moments(b, x_pre[:, b]).then_inc(s_mv[b], 1)

            def experts_norm(b):
                dve.wait_ge(s_rstd_z[b], 1)
                wait(dve, s_zT, b - 1)
                normalise(z[:, b % 2], b, x_pre[:, b], rstd_z).then_inc(s_z, 1)

            def z_lo(b):
                dve.wait_ge(s_zhi, b + 1)
                dve.tensor_tensor(xt[1][:, b * N:(b + 1) * N], bank_of(f"G{b}"), xt[0][:, b * N:(b + 1) * N].bitcast(f32),
                                  ALU.subtract).then_inc(s_zlo, 1)

            def compare_logits(b):
                dve.wait_ge(s_lg, b + 1)
                wait(dve, s_margin, b - 1)
                lg = bank_of(f"J{b}")[:, 0:JT * E].rearrange("p (j e) -> p j e", j=JT)
                dve.tensor_tensor(logits[:, b % 2], lg, rbias[:].unsqueeze(1).to_broadcast([P, JT, E]), ALU.add).then_inc(s_lgs, 1)
                dve.wait_ge(s_lgs, b + 1)
                mine = logits[:, b % 2].unsqueeze(3).to_broadcast([P, JT, E, E])
                other = logits[:, b % 2].unsqueeze(2).to_broadcast([P, JT, E, E])
                dve.tensor_tensor(pair_gt[:, b % 2], other, mine, ALU.is_gt)
                dve.tensor_tensor(pair_eq[:, b % 2], other, mine, ALU.is_equal).then_inc(s_pairs, 1)

            def gates_of_kept(b):
                dve.wait_ge(s_tanh, b + 1)
                wait(dve, s_gT, b - 1)
                dve.scalar_tensor_tensor(gates[:, b % 2], margin[:, b % 2], 1.0, half_kept[:, b % 2],
                                         op0=ALU.add, op1=ALU.mult).then_inc(s_gate, 1)

            def last_residual(b):
                dve.wait_ge(s_fT, b + 1)
                dve.wait_ge(s_x1, b + 1)
                link(dve.tensor_tensor(x_pre[:, b], tiles_of(mid_bank[b % 2]), xs[:, b * JT:(b + 1) * JT, :], ALU.add))
                moments(b, x_pre[:, b]).then_inc(s_fmv, 1)

            def last_norm(b):
                dve.wait_ge(s_frstd, b + 1)
                normalise(x_out[:, b], b, x_pre[:, b], rstd).then_inc(s_fin[b], 1)

            mid = {"C": residual, "Z": experts_norm, "G": z_lo, "J": compare_logits, "L": gates_of_kept,
                   "U": last_residual, "V": last_norm, "B": lambda _: hidden_bias(0, 0, 0)}

            def do(name):
                mid[name[0]](int(name[1]))

            def w1_hi(e, half, p):
                dve.wait_ge(s_w1_in[p], 16 * half + 16)
                dve.tensor_scalar(w1_s[p][0][:], w1_raw[p][:], scale_of(e), None, ALU.mult).then_inc(s_w1h, 1)

            def w1_lo(e, half, p):
                dve.wait_ge(s_w1h, e + 1)
                dve.scalar_tensor_tensor(w1_s[p][1][:], w1_raw[p][:], scale_of(e), w1_s[p][0][:].bitcast(f32),
                                         op0=ALU.mult, op1=ALU.subtract).then_inc(s_w1s, 1)

            def w2_lo(e, half, p):
                dve.wait_ge(s_w2hi, e + 1)
                dve.tensor_tensor(w2_s[p][1][:], w2_raw[p][:], w2_s[p][0][:].bitcast(f32), ALU.subtract).then_inc(s_w2s, 1)

            def hidden_bias(e, half, p):
                dve.wait_ge(s_lb, e + 1)
                wait(dve, s_b1, e)
                dve.tensor_reduce(w1_lb_sum[:], w1_lb[:], AX.X, ALU.add).then_inc(s_lbs, 1)
                dve.wait_ge(s_lbs, e + 1)
                b1c = cols[:, C_B1:C_B1 + E * HC].rearrange("p (e c) -> p e c", e=E)[:, e, :]
                dve.tensor_tensor(b1_s[p][:], w1_lb_sum[:], b1c, ALU.add).then_inc(s_b1, 1)

            def scale_of(e):
                return cols[:, C_LS + e:C_LS + e + 1] if isinstance(e, int) else cols[:, C_LS:C_LS + E][:, bass.ds(e, 1)]

            def after(k):
                for at, job in ((62, w1_hi), (62, w1_lo), (63, w2_lo)):
                    if k == at:
                        job(0, 0, 0)
                if k in (0, 1):
                    dve.wait_ge(s_v2, B)
                    v4 = v32[:].rearrange("p t (h e) -> p h t e", h=H)
                    hs = slice(k * H // 2, (k + 1) * H // 2)
                    dve.tensor_tensor(v_all[:, hs, :, 2 * DH:3 * DH], v4[:, hs], v_all[:, hs, :, DH:2 * DH], ALU.subtract).then_inc(s_v_all, 1)
                for name in AFTER_DVE.get(k, []):
                    do(name)

            attention_steps(dve, step, after, first=0)

            def unit_step(unit):
                work_between(unit, UNIT_DVE, LAST_DVE, do)
                v = unit.ahead(W2_LAG)
                if v.real:
                    dve.wait_ge(s_hhi, v.u + 1)
                    dve.tensor_tensor(h_lo[:, v.r % NH, :], h32[:, v.r % NH, :], h_hi[:, v.r % NH, :].bitcast(f32),
                                      ALU.subtract).then_inc(s_hlo, 1)
                if unit.r < 0:
                    return
                if has_next(unit):
                    nxt = unit.ahead(UNITS)
                    for at, job in ((PREP_W1HI, w1_hi), (PREP_W1LO, w1_lo), (PREP_W2LO, w2_lo), (PREP_B1, hidden_bias)):
                        if unit.r % UNITS == at:
                            job(nxt.expert, nxt.half, nxt.parity)
                if unit.chunk == HC - 1:
                    n = unit.expert * B + unit.tile
                    tokens = slice(unit.tile * N, (unit.tile + 1) * N)
                    dve.wait_ge(s_used, (n + 1) * HC)
                    if is_first(unit):
                        dve.tensor_scalar(acc[:, tokens], y_bank[unit.tile % 2], cols[:, C_B2:C_B2 + 1], None, ALU.add).then_inc(s_yg, 1)
                        return
                    if isinstance(unit.expert, int) and unit.expert == 1:
                        dve.wait_ge(s_gb1[unit.tile], 16)
                    elif unit.tile == 0:
                        dve.wait_ge(s_gb[unit.parity], 16 * unit.half)
                    wait(dve, s_acc, n - 1)
                    b2c = cols[:, C_B2:C_B2 + E]
                    b2c = b2c[:, unit.expert:unit.expert + 1] if isinstance(unit.expert, int) else b2c[:, bass.ds(unit.expert, 1)]
                    dve.scalar_tensor_tensor(y_g[:, unit.tile % 2, :], y_bank[unit.tile % 2], b2c, gate_b[unit.parity][:, tokens],
                                             op0=ALU.add, op1=ALU.mult).then_inc(s_yg, 1)
                    if is_end(unit):
                        dve.wait_ge(s_yg, n + 1)
                        dve.wait_ge(s_acc, n)
                        dve.tensor_tensor(acc[:, tokens], acc[:, tokens], y_g[:, unit.tile % 2, :], ALU.add).then_inc(s_acc, 1)

            expert_units(dve, unit_step)
            for name in END_DVE:
                do(name)

        @block.tensor
        def _(pe):
            def three(dst, lhs, rhs, start=True, stop=True):
                pe.matmul(dst, lhs[0], rhs[0], start=start, stop=False)
                pe.matmul(dst, lhs[0], rhs[1], start=False, stop=False)
                return pe.matmul(dst, lhs[1], rhs[0], start=False, stop=stop)

            def step(k):
                s = k.at(-1)
                if s.real:
                    pe.wait_ge(s_thi, s.g + 1)
                    wait(pe, s_max, s.g)
                    for j in reversed(range(JT)):
                        bk, at = R_AT[j]
                        pe.matmul(ps_rows[:, bk, at:at + (j + 1) * P], t_s[0][:, s.r % 4, j * P:(j + 1) * P],
                                  xt[0][:, s.b * N:s.b * N + (j + 1) * P], start=(at == 0), stop=False)
                    for j in range(JT):
                        bk, at = R_AT[j]
                        ins = pe.matmul(ps_rows[:, bk, at + j * P:at + (j + 1) * P], ident16[:], future[:], start=False, stop=(at == 0))
                    ins.then_inc(s_rowsc, 1)
                s = k.at(3)
                if s.real:
                    pe.wait_ge(s_lo, s.g + 1)
                    if s.b == 0:
                        pe.wait_ge(s_v[s.parity], 16 * s.half + 16)
                    wait(pe, s_o, s.g)
                    for j in range(JT):
                        for m in range(j + 1):
                            at = T_AT[m] + (j - m) * P
                            for part, src in enumerate((p_hi, p_lo)):
                                ins = pe.matmul(ps_o[:, j * VS:j * VS + VW], src[:, s.r % NP, at:at + P],
                                                v_cur[s.parity][:, s.b * JT + m, 0:VW], start=(m == 0 and part == 0), stop=(m == j and part == 1))
                    ins.then_inc(s_pv, 1)
                s = k.at(-2)
                if s.real:
                    if s.b == 0 and not first_head(s):
                        pe.wait_ge(s_m[s.parity], record(s))
                    wait(pe, s_tlo, s.g)
                    m = m_all[:, 0] if first_head(s) else m_cur[s.parity]
                    three(ps_t[:], [m[:, i, :] for i in range(2)], [w[:, s.b * N:(s.b + 1) * N] for w in xt]).then_inc(s_t, 1)
                s = k
                if s.real:
                    pe.wait_ge(s_tlo, s.g + 1)
                    wait(pe, s_exp, s.g)
                    tiles = diag[s.r % 2][:].rearrange("p j n -> p (j n)")
                    for key_tiles in ((0,), (1, 3), (2,)):
                        for m in key_tiles:
                            n = (JT - m) * P
                            q0 = m * P
                            three(sT[:, T_AT[m]:T_AT[m] + n], [w[:, s.b * N + q0:s.b * N + q0 + P] for w in xt],
                                  [w[:, s.r % 4, q0:N] for w in t_s], start=(m == key_tiles[0]), stop=False)
                        if 0 in key_tiles:
                            pe.wait_ge(s_diag, s.g + 1)
                        m = key_tiles[0]
                        n = sum(JT - m for m in key_tiles) * P
                        ins = pe.matmul(sT[:, T_AT[m]:T_AT[m] + n], onesr[:], tiles[:, m * P:m * P + n], start=False, stop=True)
                    ins.then_inc(s_sT, 1)

            pe.wait_ge(s_const, 1)
            for n in range(JOBS):
                if n == J_B:
                    pe.wait_ge(s_sact, act_done(0))
                    pe.wait_ge(s_sdve, dve_done(0))
                elif n == J_V:
                    pe.wait_ge(s_sact, act_done(J_B - 1))
                    pe.wait_ge(s_sdve, dve_done(J_B - 1))
                elif n >= J_V + 4:
                    pe.wait_ge(s_sdve, dve_done(n - 4))
                bk = banks[n % 8 if n < J_V else V_BANKS[(n - J_V) % 4]]
                if n < J_B:
                    if n % 4 == 0:
                        pe.wait_ge(s_w_in[n // 4], 32)
                    for a in range(2):
                        ins = pe.matmul(bk[:, a * 256:a * 256 + D + 1], wqT[:, 2 * n + a, :], wkT[:, 2 * n + a, :], start=True, stop=True)
                elif n == J_B:
                    pe.wait_ge(s_rw, 1)
                    for h in range(H):
                        pe.matmul(bk[:, h:h + 1], wkT[:, h, 0:D], cols[:, C_BQ + h:C_BQ + h + 1], start=True, stop=True)
                    pe.matmul(bk[:, H:2 * H], ones[:], bias_prod[:], start=True, stop=True)
                    ins = pe.matmul(bk[:, 2 * H:2 * H + E], rlb_b[:], cols[:, C_RW:C_RW + E], start=True, stop=True)
                else:
                    i = n - J_V
                    if i == 0:
                        pe.wait_ge(s_wv_in, 16)
                        pe.wait_ge(s_vcw, 1)
                    pe.wait_ge(s_xlo, 2 * i // JT + 1)
                    for a in range(2):
                        t = 2 * i + a
                        for part in range(2):
                            ins = pe.matmul(bk[:, a * 256:a * 256 + VC], xt[part][:, t * P:(t + 1) * P].bitcast(f32), vc32[:],
                                            start=(part == 0), stop=(part == 1))
                ins.then_inc(s_fill, 1)
                if n == J_V:
                    pe.wait_ge(s_sact, act_done(J_B))
                    pe.wait_ge(s_sdve, dve_done(J_B))
                if n - J_V in EARLY_PE:
                    step(Step(0, EARLY_PE[n - J_V]))

            pe.wait_ge(s_sdve, dve_done(JOBS - 1))

            def transpose_sa(b, bk):
                pe.wait_ge(s_sa, G - B + b + 1)
                for j in range(JT):
                    ins = pe.transpose(bk[:, j * P:(j + 1) * P], sa_all[:, b * JT + j, :], ident[:])
                ins.then_inc(s_saT_ps, 1)

            def project(b, bk):
                pe.wait_ge(s_wp_in, 16)
                pe.wait_ge(s_saT, b + 1)
                for j in range(JT):
                    ins = pe.matmul(bk[:, j * P:(j + 1) * P], saT[:, b % 2, j * P:(j + 1) * P], wp_s[:], start=True, stop=True)
                ins.then_inc(s_att, 1)

            def transpose_z(b, bk):
                pe.wait_ge(s_z, b + 1)
                for j in range(JT):
                    ins = pe.transpose(bk[:, j * P:(j + 1) * P], z[:, b % 2, j, :], ident[:])
                ins.then_inc(s_zT, 1)

            def router(b, bk):
                pe.wait_ge(s_zlo, b + 1)
                for j in range(JT):
                    t = b * JT + j
                    for i in range(2):
                        ins = pe.matmul(bk[:, j * E:(j + 1) * E], xt[i][:, t * P:(t + 1) * P].bitcast(f32), rw_s[:], start=(i == 0), stop=(i == 1))
                ins.then_inc(s_lg, 1)

            def transpose_gates(b, bk):
                pe.wait_ge(s_gate, b + 1)
                for j in range(JT):
                    ins = pe.transpose(bk[0:E, j * P:(j + 1) * P], gates[:, b % 2, j, :], ident[:])
                ins.then_inc(s_gT, 1)

            def transpose_out(b):
                pe.wait_ge(s_acc, (E - 1) * B + b + 1)
                if b >= 2:
                    pe.wait_ge(s_fmv, b - 1)
                for j in range(JT):
                    t = b * JT + j
                    ins = pe.transpose(mid_bank[b % 2][:, j * P:(j + 1) * P], acc[:, t * P:(t + 1) * P], ident[:])
                ins.then_inc(s_fT, 1)

            stage = {"A": transpose_sa, "G": transpose_z, "J": router, "M": transpose_gates}

            def mid(name):
                if name[0] == "T":
                    return transpose_out(int(name[1]))
                if name[0] == "C":
                    pe.wait_ge(s_max, G)
                    if name[1] != "0":
                        pe.wait_ge(s_exp, G)
                    return project(int(name[1]), bank_of(name))
                n = mid_order.index(name)
                if n >= 2:
                    before = mid_order[n - 2]
                    pe.wait_ge(mid_reader[before[0]], int(before[1]) + 1)
                else:
                    pe.wait_ge(s_max, G)
                stage[name[0]](int(name[1]), bank_of(name))

            def after(k):
                for name in AFTER_PE.get(k, []):
                    mid(name)

            attention_steps(pe, step, after, first=0)
            pe.wait_ge(s_o, G)

            def unit_step(unit):
                work_between(unit, UNIT_PE, LAST_PE, mid)
                if isinstance(unit.rounds, int) and unit.u == -1:
                    pe.wait_ge(s_xpre, B)
                v = unit.ahead(W2_LAG)
                if v.real:
                    if v.r % UNITS == 0:
                        pe.wait_ge(s_w1s, v.expert + 1)
                    if is_first(v) and v.chunk == 0:
                        pe.wait_ge(s_zlo, v.tile + 1)
                    wait(pe, s_g, v.u - PH + 1)
                    c, t0 = v.chunk, v.tile * N
                    three(hid_bank_of(v), [w[:, c * P:(c + 1) * P] for w in w1_s[v.parity]], [w[:, t0:t0 + N] for w in xt]).then_inc(s_h, 1)
                if unit.r < 0:
                    return
                if unit.r % UNITS == 0:
                    pe.wait_ge(s_w2s, unit.expert + 1)
                pe.wait_ge(s_hlo, unit.u + 1)
                n = unit.expert * B + unit.tile
                if unit.chunk == 0:
                    wait(pe, s_yg, n - 1)
                ins = three(y_bank[unit.tile % 2], [w[:, unit.chunk, :] for w in w2_s[unit.parity]],
                            [w[:, unit.r % NH, :] for w in (h_hi, h_lo)], start=(unit.chunk == 0), stop=(unit.chunk == HC - 1))
                ins.then_inc(s_used, 1)

            expert_units(pe, unit_step)
            for name in END_PE:
                mid(name)


def lay_out(i):
    wkqv, bkqv = i["L0_attn_Wkqv"], i["L0_attn_bkqv"]
    wk, wq, wv = wkqv[:, :, 0:D], wkqv[:, :, D:2 * D], wkqv[:, :, 2 * D:]
    bk, bq, bv = bkqv[:, 0:D], bkqv[:, D:2 * D], bkqv[:, 2 * D:]
    columns = [bk.T, bq.T, i["L0_ffn_expert_ln_scale"].T, i["L0_ffn_b2"].T, i["L0_ffn_b1"].reshape(E * HC, P).T,
               i["L0_ffn_router_ln_bias"][:, None], i["L0_ffn_router_ln_scale"][:, None], i["L0_ffn_router_w"].T]
    return {
        "x": i["L0_attn_x"],
        "xT": i["L0_attn_x"].reshape(T, D).T,
        "wkT": np.concatenate([wk.transpose(2, 0, 1), bk.T[:, :, None]], axis=2),
        "wqT": wq.transpose(2, 0, 1),
        "wv": wv.transpose(1, 0, 2).reshape(D, H * DH),
        "wp": i["L0_attn_Wp"],
        "columns": np.concatenate(columns, axis=1),
        "rows": np.concatenate([bv.reshape(-1), i["L0_attn_bp"], i["L0_ffn_router_b"]]),
        "expert_ln_bias": i["L0_ffn_expert_ln_bias"],
        "w1": i["L0_ffn_w1"],
        "w1T": i["L0_ffn_w1"].transpose(0, 2, 1),
        "w2T": i["L0_ffn_w2"].transpose(0, 2, 1),
    }


def kernel(**inputs):
    import numpy as _np
    import concourse.bacc as _bacc
    from concourse import mybir as _mybir
    from concourse.bass_utils import run_bass_kernel_spmd as _run

    nc = _bacc.Bacc("TRN2", target_bir_lowering=False, num_devices=1)
    arrays, args = {}, []
    for name, a in lay_out({n: _np.asarray(v) for n, v in inputs.items()}).items():
        a = _np.ascontiguousarray(a)
        arrays[f"in_{name}"] = a
        args.append(nc.dram_tensor(f"in_{name}", a.shape, _mybir.dt.from_np(a.dtype), kind="ExternalInput").ap())
    args.append(nc.dram_tensor("out", (B, N, D), _mybir.dt.float32, kind="ExternalOutput").ap())
    post_ln_layer(nc, *args)
    r = _run(nc, [arrays], core_ids=[0])
    return r.results[0]["out"]
```
